# Optimizing a Trainium2 kernel written in Bass

```python
import numpy as np
import jax
import jax.numpy as jnp

def _softmax(x, axis=-1):
    return jax.nn.softmax(x, axis=axis)

def _gelu(x):
    return jax.nn.gelu(x, approximate=True)

def _silu(x):
    return jax.nn.silu(x)

def _sigmoid(x):
    return jax.nn.sigmoid(x)

def _layernorm(x, axis=-1, eps=1e-05):
    m = jnp.mean(x, axis=axis, keepdims=True)
    v = jnp.var(x, axis=axis, keepdims=True)
    return (x - m) / jnp.sqrt(v + eps)

def _scatter_add(tgt, idx, src, axis=0):
    return tgt.at[idx].add(src)

def _segment_sum(src, seg, n):
    return jax.ops.segment_sum(src, seg, n)
kernel_name = 'mk_hybrid_d1_jaxref_r8_bfaee2'

def setup_inputs(seed: int=0):
    np.random.seed(seed)
    _w = jnp.asarray

    def _L0_attn_a_setup():
        import jax, jax.numpy as jnp
        import numpy as np
        B, S, HID, NH = (8, 512, 128, 16)
        D = HID // NH
        LN_EPS = 1e-05

        def _l2norm(a):
            n = jnp.sqrt(jnp.sum(a * a, axis=-1, keepdims=True))
            return a / jnp.maximum(n, 1e-12)
        key = jax.random.key(seed)
        ks = jax.random.split(key, 8)
        s = 0.02
        x = jax.random.normal(ks[0], (B, S, HID), jnp.float32)
        Wq = jax.random.normal(ks[1], (HID, NH * D), jnp.float32) * s
        Wk = jax.random.normal(ks[2], (HID, NH * D), jnp.float32) * s
        Wv = jax.random.normal(ks[3], (HID, NH * D), jnp.float32) * s
        Wbeta = jax.random.normal(ks[4], (HID, NH), jnp.float32) * s
        Wg = jax.random.normal(ks[5], (HID, NH * D), jnp.float32) * s
        Wout = jax.random.normal(ks[6], (NH * D, HID), jnp.float32) * s
        ln_g = jnp.ones((NH * D,), jnp.float32)
        ln_b = jnp.zeros((NH * D,), jnp.float32)
        return {'x': x, 'Wq': Wq, 'Wk': Wk, 'Wv': Wv, 'Wbeta': Wbeta, 'Wg': Wg, 'Wout': Wout, 'ln_g': ln_g, 'ln_b': ln_b}
    _L0_attn_a_in = _L0_attn_a_setup()

    def _L0_attn_b_setup():
        import jax, jax.numpy as jnp
        import numpy as np
        B, N, D = (4, 512, 128)
        H, F = (16, 128)
        HD = D // H
        key = jax.random.key(seed)
        k1, k2, k3, k4, k5 = jax.random.split(key, 5)
        x = jax.random.normal(k1, (B, N, D), dtype=jnp.float32)
        W_qkv = jax.random.normal(k2, (3 * D, D), dtype=jnp.float32) * np.sqrt(2.0 / D)
        proj = jax.random.normal(k3, (H, HD, F), dtype=jnp.float32) / np.sqrt(HD)
        W_out = jax.random.normal(k4, (D, D), dtype=jnp.float32) * np.sqrt(2.0 / D)
        b_out = jnp.zeros((D,), dtype=jnp.float32)
        return {'x': x, 'W_qkv': W_qkv, 'proj': proj, 'W_out': W_out, 'b_out': b_out}
    _L0_attn_b_in = _L0_attn_b_setup()

    def _L0_ffn_setup():
        import jax, jax.numpy as jnp
        import numpy as np
        import math
        N_EXP = 8
        TOP_K = 2
        CAPACITY_FACTOR = 1.25

        def _capacity(num_tokens):
            cap = math.floor(TOP_K * CAPACITY_FACTOR * num_tokens / N_EXP)
            cap += cap % 2
            return int(cap)
        key = jax.random.key(seed)
        k1, k2, k3, k4 = jax.random.split(key, 4)
        B, C, d = (4, 128, 128)
        x = jax.random.normal(k1, (B, C, d), dtype=jnp.float32)
        w_g = jax.random.normal(k2, (d, N_EXP), dtype=jnp.float32) * 0.02
        c_fc = jax.random.normal(k3, (N_EXP, d, 4 * d), dtype=jnp.float32) * 0.02
        c_proj = jax.random.normal(k4, (N_EXP, 4 * d, d), dtype=jnp.float32) * 0.02
        return {'x': x, 'w_g': w_g, 'c_fc': c_fc, 'c_proj': c_proj}
    _L0_ffn_in = _L0_ffn_setup()
    _d = {'L0_attn_a_x': _L0_attn_a_in['x'], 'L0_attn_a_Wq': _L0_attn_a_in['Wq'], 'L0_attn_a_Wk': _L0_attn_a_in['Wk'], 'L0_attn_a_Wv': _L0_attn_a_in['Wv'], 'L0_attn_a_Wbeta': _L0_attn_a_in['Wbeta'], 'L0_attn_a_Wg': _L0_attn_a_in['Wg'], 'L0_attn_a_Wout': _L0_attn_a_in['Wout'], 'L0_attn_a_ln_g': _L0_attn_a_in['ln_g'], 'L0_attn_a_ln_b': _L0_attn_a_in['ln_b'], 'L0_attn_b_W_qkv': _L0_attn_b_in['W_qkv'], 'L0_attn_b_proj': _L0_attn_b_in['proj'], 'L0_attn_b_W_out': _L0_attn_b_in['W_out'], 'L0_attn_b_b_out': _L0_attn_b_in['b_out'], 'L0_ffn_w_g': _L0_ffn_in['w_g'], 'L0_ffn_c_fc': _L0_ffn_in['c_fc'], 'L0_ffn_c_proj': _L0_ffn_in['c_proj']}
    _x0 = _d['L0_attn_a_x']
    _d['L0_attn_a_x'] = jax.random.normal(jax.random.fold_in(jax.random.key(seed), 1), (1, 2048, 128), dtype=_x0.dtype)
    del _x0
    return _d

def reference(L0_attn_a_x, L0_attn_a_Wq, L0_attn_a_Wk, L0_attn_a_Wv, L0_attn_a_Wbeta, L0_attn_a_Wg, L0_attn_a_Wout, L0_attn_a_ln_g, L0_attn_a_ln_b, L0_attn_b_W_qkv, L0_attn_b_proj, L0_attn_b_W_out, L0_attn_b_b_out, L0_ffn_w_g, L0_ffn_c_fc, L0_ffn_c_proj):

    def _L0_attn_a_ref(x, Wq, Wk, Wv, Wbeta, Wg, Wout, ln_g, ln_b):
        import jax, jax.numpy as jnp
        import numpy as np
        B, S, HID, NH = (8, 512, 128, 16)
        D = HID // NH
        LN_EPS = 1e-05

        def _l2norm(a):
            n = jnp.sqrt(jnp.sum(a * a, axis=-1, keepdims=True))
            return a / jnp.maximum(n, 1e-12)
        b, s, _ = x.shape
        nh = Wbeta.shape[1]
        d = Wq.shape[1] // nh
        q = _l2norm((x @ Wq).reshape(b, s, nh, d))
        k = _l2norm((x @ Wk).reshape(b, s, nh, d))
        v = (x @ Wv).reshape(b, s, nh, d)
        beta = jax.nn.sigmoid(x @ Wbeta)
        qT = jnp.moveaxis(q, 1, 0)
        kT = jnp.moveaxis(k, 1, 0)
        vT = jnp.moveaxis(v, 1, 0)
        bT = jnp.moveaxis(beta, 1, 0)
        state0 = jnp.zeros((b, nh, d, d), x.dtype)

        def step(state, inp):
            qt, kt, vt, bt = inp
            kk = kt[..., :, None] * kt[..., None, :]
            bb = bt[..., None, None]
            state = state * (1.0 - bb * kk) + bb * (vt[..., :, None] * kt[..., None, :])
            out_t = jnp.einsum('bhij,bhj->bhi', state, qt)
            return (state, out_t)
        _, outs = jax.lax.scan(step, state0, (qT, kT, vT, bT))
        out = jnp.moveaxis(outs, 0, 1).reshape(b, s, nh * d)
        mu = jnp.mean(out, axis=-1, keepdims=True)
        var = jnp.mean((out - mu) ** 2, axis=-1, keepdims=True)
        out = (out - mu) / jnp.sqrt(var + LN_EPS) * ln_g + ln_b
        out = out * jax.nn.silu(x @ Wg)
        return out @ Wout

    def _L0_attn_b_ref(x, W_qkv, proj, W_out, b_out):
        import jax, jax.numpy as jnp
        import numpy as np
        B, N, D = (4, 512, 128)
        H, F = (16, 128)
        HD = D // H
        b, n, d = x.shape
        qkv = x @ W_qkv.T
        q, k, v = jnp.split(qkv, 3, axis=-1)
        reshp = lambda t: t.reshape(b, n, H, HD).transpose(0, 2, 1, 3)
        q, k, v = (reshp(q), reshp(k), reshp(v))
        q_p = jax.nn.elu(jnp.einsum('bhnd,hdf->bhnf', q, proj)) + 1.0
        k_p = jax.nn.elu(jnp.einsum('bhnd,hdf->bhnf', k, proj)) + 1.0
        kv = jnp.einsum('bhnf,bhnd->bhfd', k_p, v)
        attn = jnp.einsum('bhnf,bhfd->bhnd', q_p, kv)
        k_sum = k_p.sum(axis=2)
        z = 1.0 / (jnp.einsum('bhnf,bhf->bhn', q_p, k_sum) + 1e-08)
        attn = attn * z[..., None]
        attn = attn.transpose(0, 2, 1, 3).reshape(b, n, d)
        return attn @ W_out.T + b_out

    def _L0_ffn_ref(x, w_g, c_fc, c_proj):
        import jax, jax.numpy as jnp
        import numpy as np
        import math
        N_EXP = 8
        TOP_K = 2
        CAPACITY_FACTOR = 1.25

        def _capacity(num_tokens):
            cap = math.floor(TOP_K * CAPACITY_FACTOR * num_tokens / N_EXP)
            cap += cap % 2
            return int(cap)
        B, C, d = x.shape
        T = B * C
        cap = _capacity(T)
        xt = x.reshape(T, d)
        logits = xt @ w_g
        top_v, top_i = jax.lax.top_k(logits, TOP_K)
        full = jnp.full_like(logits, -jnp.inf)
        full = full.at[jnp.arange(T)[:, None], top_i].set(top_v)
        probs = jax.nn.softmax(full, axis=-1)
        exp_mask = jax.nn.one_hot(top_i, N_EXP, dtype=jnp.int32)
        exp_mask = jnp.transpose(exp_mask, (1, 0, 2))
        exp_rank = jnp.cumsum(exp_mask.reshape(TOP_K * T, N_EXP), axis=0) - 1
        exp_rank = exp_rank.reshape(TOP_K, T, N_EXP)
        exp_mask = exp_mask * (exp_rank < cap).astype(jnp.int32)
        exp_rank = jnp.sum(exp_mask * exp_rank, axis=-1)
        exp_weights = exp_mask.astype(x.dtype) * probs[None]
        rank_oh = jax.nn.one_hot(exp_rank, cap, dtype=x.dtype)
        cb_weight = jnp.einsum('kte,ktc->tec', exp_weights, rank_oh)
        sec_mask = (cb_weight != 0).astype(x.dtype)
        exp_batches = jnp.einsum('tec,td->ecd', sec_mask, xt)
        h = jax.nn.gelu(jnp.einsum('ecd,edf->ecf', exp_batches, c_fc), approximate=False)
        exp_out = jnp.einsum('ecf,efd->ecd', h, c_proj)
        out = cb_weight.reshape(T, N_EXP * cap) @ exp_out.reshape(N_EXP * cap, d)
        return out.reshape(B, C, d)
    x = L0_attn_a_x
    x = x + _L0_attn_a_ref(_layernorm(x, axis=-1), L0_attn_a_Wq, L0_attn_a_Wk, L0_attn_a_Wv, L0_attn_a_Wbeta, L0_attn_a_Wg, L0_attn_a_Wout, L0_attn_a_ln_g, L0_attn_a_ln_b)
    x = x + _L0_ffn_ref(_layernorm(x, axis=-1), L0_ffn_w_g, L0_ffn_c_fc, L0_ffn_c_proj)
    x = x + _L0_attn_b_ref(_layernorm(x, axis=-1), L0_attn_b_W_qkv, L0_attn_b_proj, L0_attn_b_W_out, L0_attn_b_b_out)
    x = x + _L0_ffn_ref(_layernorm(x, axis=-1), L0_ffn_w_g, L0_ffn_c_fc, L0_ffn_c_proj)
    return x

_drawn_inputs = setup_inputs


def setup_inputs(seed=0):
    import zlib

    import numpy as np

    out = dict(_drawn_inputs(seed))
    spreads = {'L0_attn_a_ln_g': (1.0, 0.6), 'L0_attn_a_ln_b': (0.0, 2.0), 'L0_attn_b_b_out': (0.0, 0.1)}
    factors = {'L0_attn_a_Wv': 2.799, 'L0_attn_a_Wbeta': 23.841, 'L0_attn_b_proj': 3.14}
    for name, (base, spread) in spreads.items():
        noise = np.random.default_rng([zlib.crc32(name.encode()), seed]).standard_normal(out[name].shape)
        drawn = base * np.exp(spread * noise) if base else spread * noise
        out[name] = jnp.asarray(drawn.astype(out[name].dtype))
    for name, factor in factors.items():
        out[name] = (out[name] * factor).astype(out[name].dtype)
    return out
```

```python
from contextlib import ExitStack

import concourse.bass as bass
from concourse import mybir

F32 = mybir.dt.float32
F32R = mybir.dt.float32r
BF16 = mybir.dt.bfloat16
I32 = mybir.dt.int32
ALU = mybir.AluOpType
ACT = mybir.ActivationFunctionType
AX_X = mybir.AxisListType.X

P = 128
TOK = 2048
D = 128
NT = TOK // P
H = 16
HD = D // H
EPS = 1e-5
BK = 512
NB = TOK // BK
TB = BK // P

QKVB = 3 * D + H
CH = 1024
NCH = TOK // CH

NE = 8
FF = 4 * D
NF = FF // P
CAP = 640
NS = CAP // P
HALF = CAP // 2
KT = 2 * NT
FAR = 65536.0

NG = 4
GH = H // NG
GR = GH * HD
STK = 3 * GR + 1
F = 128


def program(nc, x, Wq, Wk, Wv, Wbeta, Wg, Wout, ln_g, ln_b, W_qkv, proj, W_out, b_out, w_g, c_fc, c_proj, out):
    ctx = ExitStack()

    def sb(name, shape, dt=F32, stack=None):
        return (stack or ctx).enter_context(nc.sbuf_tensor(name, shape, dt))

    def sem(name):
        return ctx.enter_context(nc.semaphore(name))

    with ctx:
        ps = ctx.enter_context(nc.psum_tensor("ps", [P, 8, BK], F32))
        xres = sb("xres", [P, NT, D])
        xn = sb("xn", [P, NT, D])
        xnT = sb("xnT", [P, TOK])
        ident = sb("ident", [P, P])
        ones_bf = sb("ones_bf", [P, P], BF16)
        before_bf = sb("before_bf", [P, P], BF16)
        first_tile = sb("first_tile", [P, NE, KT])
        expert_base = sb("expert_base", [P, NE, KT])
        low_first = sb("low_first", [P, NT, NE])
        minus_one = sb("minus_one", [P, 1])
        eps_col = sb("eps_col", [P, 1])
        ones_row = sb("ones_row", [1, P])
        stats = sb("stats", [P, NT, 6])
        mv = sb("mv", [P, NT, 2])
        std = sb("std", [P, NT])
        rstd = sb("rstd", [P, NT])
        wg_sb = sb("wg_sb", [P, NE])
        cproj_sb = sb("cproj_sb", [P, NE, NF, D])
        bout_row = sb("bout_row", [1, D])
        zero_rows = sb("zero_rows", [P, NS * D])
        wvT = sb("wvT", [P, D])
        wkT = sb("wkT", [P, D])
        wqT = sb("wqT", [P, D])
        woT = sb("woT", [P, D])
        slots_x = nc.dram_tensor("slots_x", [NE * CAP, D], F32).ap()
        slots_y = nc.dram_tensor("slots_y", [NE * CAP, D], F32).ap()

        with ExitStack() as a:
            wall = sb("wall", [P, QKVB], F32, a)
            wgate = sb("wgate", [P, D], F32, a)
            wout = sb("wout", [P, D], F32, a)
            lng = sb("lng", [P, 1], F32, a)
            lnb = sb("lnb", [P, 1], F32, a)
            wnat = sb("wnat", [P, 4, D], F32, a)
            sel_f = sb("sel_f", [P, HD, P], F32, a)
            sel = sb("sel", [P, HD, P], F32R, a)
            headsum = sb("headsum", [P, 32], F32, a)
            qT = sb("qT", [P, TOK], F32, a)
            bkT = sb("bkT", [P, TOK], F32, a)
            with ExitStack() as a1:
                khi = sb("khi", [P, TOK], F32R, a1)
                klo = sb("klo", [P, TOK], F32R, a1)
                vhi = sb("vhi", [P, TOK], F32R, a1)
                vlo = sb("vlo", [P, TOK], F32R, a1)
                with ExitStack() as a2:
                    raw = sb("raw", [P, NT, QKVB], F32, a2)
                    squares = sb("squares", [P, NT, 2 * D], F32, a2)
                    norm = sb("norm", [P, NT, 2 * H], F32, a2)
                    rnorm = sb("rnorm", [P, NT, 2 * H], F32, a2)
                    beta = sb("beta", [P, NT, H], F32, a2)
                    bk = sb("bk", [P, NT, D], F32, a2)
                with ExitStack() as a3:
                    decay = sb("decay", [P, 2, CH], F32, a3)
                    update = sb("update", [P, 2, CH], F32, a3)
                    state = sb("state", [P, HD, CH], F32, a3)
                    read = sb("read", [P, HD, CH], F32, a3)
                    oT = sb("oT", [P, 2, TOK], F32, a3)
            with ExitStack() as a4:
                otok = sb("otok", [P, NT, D], F32, a4)
                gated = sb("gated", [P, TOK], F32, a4)

        with ExitStack() as m:
            cfc_sb = sb("cfc_sb", [P, NE, FF], F32, m)
            lg = sb("lg", [P, NT, NE], F32, m)
            lg2 = sb("lg2", [P, NT, NE], F32, m)
            ranked = sb("ranked", [P, NT, NE], F32, m)
            top = sb("top", [P, 2, NT], F32, m)
            best = sb("best", [P, 2, NT], F32, m)
            gap = sb("gap", [P, NT], F32, m)
            prob = sb("prob", [P, KT], F32, m)
            chosen = sb("chosen", [P, NE, KT], F32, m)
            chosen_bf = sb("chosen_bf", [P, NE * KT], BF16, m)
            upto = sb("upto", [P, NE * KT], F32, m)
            table = sb("table", [P, NE, KT], F32, m)
            table2 = sb("table2", [P, NE, KT], F32, m)
            rank = sb("rank", [P, KT], F32, m)
            base = sb("base", [P, KT], F32, m)
            kept = sb("kept", [P, KT], F32, m)
            slot = sb("slot", [P, KT], F32, m)
            slot2 = sb("slot2", [P, KT], F32, m)
            put_at = sb("put_at", [P, KT], I32, m)
            get_at = sb("get_at", [P, KT], I32, m)
            weight = sb("weight", [P, KT], F32, m)
            xe = sb("xe", [P, 2, NS, D], F32, m)
            xeT = sb("xeT", [P, 2, CAP], F32, m)
            wfc = sb("wfc", [P, 2, FF], F32, m)
            hT = sb("hT", [P, 2, NF, CAP], F32, m)
            ye = sb("ye", [P, 2, NS * D], F32, m)
            got = sb("got", [P, KT, D], F32, m)

        with ExitStack() as b:
            projf = sb("projf", [3 * GR, NG, BK], F32, b)
            pstk = sb("pstk", [STK, NG, BK], F32R, b)
            kstk = sb("kstk", [STK, NG, TOK], F32R, b)
            qstk = sb("qstk", [STK, NG, TOK], F32R, b)
            part_hi = sb("part_hi", [P, TOK], F32R, b)
            part_lo = sb("part_lo", [P, TOK], F32R, b)
            vaug = sb("vaug", [P, NT, NG, GR + 1], F32, b)
            expo = sb("expo", [P, 3, 2 * BK], F32, b)
            feat = sb("feat", [P, 3, 2 * BK], F32, b)
            kv_sb = sb("kv_sb", [P, 2, BK], F32, b)
            kvl = sb("kvl", [P, H, 64], F32, b)
            at_sb = sb("at_sb", [P, 2, BK], F32, b)
            den = sb("den", [P, TB, H], F32, b)
            rden = sb("rden", [P, TB, H], F32, b)
            att = sb("att", [P, TB, D], F32, b)
            attT = sb("attT", [P, BK], F32, b)

        x_in = [sem(f"x_in{c}") for c in range(NB)]
        w_in = sem("w_in")
        wnat_in = sem("wnat_in")
        cproj_in = sem("cproj_in")
        cfc_in = sem("cfc_in")
        proj_in = sem("proj_in")
        zeroed = sem("zeroed")
        const_made = sem("const_made")
        sel_made = sem("sel_made")
        slots_clear = sem("slots_clear")
        ln_stat, ln_mv, ln_std, ln_rstd, ln_out = (sem(n) for n in ("ln_stat", "ln_mv", "ln_std", "ln_rstd", "ln_out"))
        xn_turned, xnT_ready = sem("xn_turned"), sem("xnT_ready")
        wT_mm, wT_ready = sem("wT_mm"), sem("wT_ready")
        qkv_mm, raw_ready, sq_ready, sumsq, norm_ready = (
            sem(n) for n in ("qkv_mm", "raw_ready", "sq_ready", "sumsq", "norm_ready"))
        rn_clamped, rn_ready, unit_ready, beta_ready, bk_ready = (
            sem(n) for n in ("rn_clamped", "rn_ready", "unit_ready", "beta_ready", "bk_ready"))
        qkv_turned, hi_ready, lo_ready = sem("qkv_turned"), sem("hi_ready"), sem("lo_ready")
        carry_zero = sem("carry_zero")
        krep_ready, krep_used, vrep_ready, update_ready = (
            sem(n) for n in ("krep_ready", "krep_used", "vrep_ready", "update_ready"))
        decay_ready, scan_done, read_ready, out_ready, oT_ready = (
            sem(n) for n in ("decay_ready", "scan_done", "read_ready", "out_ready", "oT_ready"))
        o_turned, otok_ready, gate_mm, gate_ready, nT_ready, gated_ready, y_mm = (
            sem(n) for n in ("o_turned", "otok_ready", "gate_mm", "gate_ready", "nT_ready", "gated_ready", "y_mm"))
        xres_a = sem("xres_a")
        logit_mm, logit_ready, route_step, prob_ready = (
            sem(n) for n in ("logit_mm", "logit_ready", "route_step", "prob_ready"))
        chosen_ready, count_mm, index_ready, weight_ready, scattered = (
            sem(n) for n in ("chosen_ready", "count_mm", "index_ready", "weight_ready", "scattered"))
        xe_in = [sem(f"xe_in{i}") for i in range(2)]
        ye_out = [sem(f"ye_out{i}") for i in range(2)]
        xe_turned, xeT_ready, wfc_ready, h_mm, h_ready, ye_mm, ye_ready = (
            sem(n) for n in ("xe_turned", "xeT_ready", "wfc_ready", "h_mm", "h_ready", "ye_mm", "ye_ready"))
        gathered = [sem(f"gathered{t}") for t in range(NT)]
        mix_first = sem("mix_first")
        gap_ready, pstklo_ready = sem("gap_ready"), sem("pstklo_ready")
        mixed = sem("mixed")
        qkv2_mm, v2_ready, part_ready, partlo_ready, stk_in = (
            sem(n) for n in ("qkv2_mm", "v2_ready", "part_ready", "partlo_ready", "stk_in"))
        pstk_ready, ones_made = sem("pstk_ready"), sem("ones_made")
        kf_mm, kf_exp, kf_ready, kv_mm = (sem(n) for n in ("kf_mm", "kf_exp", "kf_ready", "kv_mm"))
        kv_copied, kv_turned, kvl_ready = sem("kv_copied"), sem("kv_turned"), sem("kvl_ready")
        qf_mm, qf_exp, qf_ready, at_mm = (sem(n) for n in ("qf_mm", "qf_exp", "qf_ready", "at_mm"))
        at_ready, at_turned, den_ready, rden_ready, att_ready, att_turned, attT_ready, o2_mm, xres_b = (
            sem(n) for n in ("at_ready", "at_turned", "den_ready", "rden_ready", "att_ready", "att_turned",
                             "attT_ready", "o2_mm", "xres_b"))
        stored = sem("stored")

        N_CONST = 5
        block = ctx.enter_context(nc.Block())
        x_t = x.rearrange("a (t p) d -> p (a t) d", p=P)
        out_t = out.rearrange("a (t p) d -> p (a t) d", p=P)
        flat = lambda ap: ap.rearrange("p a b -> p (a b)")

        @block.sync
        def _(sp):
            for c in range(NB):
                sp.dma_start(xres[:, TB * c:TB * c + TB, :], x_t[:, TB * c:TB * c + TB, :]).then_inc(x_in[c], 16)
            for n, w in enumerate((Wq, Wk, Wv)):
                sp.dma_start(wall[:, n * D:(n + 1) * D], w).then_inc(w_in, 16)
            sp.dma_start(wall[:, 3 * D:QKVB], Wbeta).then_inc(w_in, 16)
            sp.dma_start(wnat[:, 0:3, :], W_qkv.rearrange("(n p) d -> p n d", p=P)).then_inc(wnat_in, 16)
            sp.dma_start(wnat[:, 3, :], W_out).then_inc(wnat_in, 16)
            sp.dma_start(wgate[:], Wg).then_inc(w_in, 16)
            sp.dma_start(wout[:], Wout).then_inc(w_in, 16)
            sp.dma_start(lng[:], ln_g.rearrange("(p a) -> p a", a=1)).then_inc(w_in, 16)
            sp.dma_start(lnb[:], ln_b.rearrange("(p a) -> p a", a=1)).then_inc(w_in, 16)
            sp.dma_start(wg_sb[:], w_g).then_inc(w_in, 16)
            sp.dma_start(bout_row[:], b_out.rearrange("(a d) -> a d", a=1)).then_inc(w_in, 16)
            sp.dma_start(cproj_sb[:], c_proj.rearrange("e (c p) d -> p e c d", p=P)).then_inc(cproj_in, 16)
            sp.wait_ge(zeroed, 1)
            for e in range(NE):
                sp.dma_start(slots_x[e * CAP:(e + 1) * CAP, :].rearrange("(p s) d -> p (s d)", s=NS),
                             zero_rows[:]).then_inc(slots_clear, 16)

            def experts(k):
                if k == 0:
                    sp.wait_ge(xres_a, NB)
                else:
                    sp.wait_ge(xres_b, NB + 1)
                sp.dma_start(cfc_sb[:], c_fc.rearrange("e d f -> d e f")).then_inc(cfc_in, 16)
                sp.wait_ge(scattered, 16 * KT * (k + 1))

                def load(e, b):
                    sp.dma_start(xe[:, b, :, :].rearrange("p s d -> p (s d)"),
                                 slots_x[bass.ds(e * CAP, CAP), :].rearrange("(p s) d -> p (s d)", s=NS)
                                 ).then_inc(xe_in[b], 16)

                def store(e, b, seq):
                    sp.wait_ge(ye_ready, seq + 1)
                    sp.dma_start(slots_y[bass.ds(e * CAP, CAP), :].rearrange("(p s) d -> p (s d)", s=NS),
                                 ye[:, b, :]).then_inc(ye_out[b], 16)

                for b in range(2):
                    load(b, b)
                with sp.Fori(0, NE // 2 - 1) as pair:
                    for b in range(2):
                        e = pair * 2
                        store(e + b, b, k * NE + e + b + 1)
                        sp.wait_ge(xe_turned, k * NE + e + b + 1)
                        load(e + b + 2, b)
                for b in range(2):
                    store(NE - 2 + b, b, k * NE + NE - 1 + b)

            experts(0)
            sp.wait_ge(mixed, NT)
            sp.wait_ge(zeroed, 2)
            for r in range(3):
                for a_ in range(GH):
                    row = GR * r + HD * a_
                    sp.dma_start(projf[row:row + HD, :, a_ * F:(a_ + 1) * F],
                                 proj.rearrange("(g a) d f -> a d g f", a=GH)[a_]).then_inc(proj_in, 16)
            for n, stk in enumerate((kstk, qstk)):
                sp.wait_ge(part_ready, NB * (n + 1))
                sp.wait_ge(partlo_ready, NB * (n + 1))
                for g in range(NG):
                    for r, part in enumerate((part_hi, part_lo, part_hi)):
                        sp.dma_start(stk[GR * r:GR * (r + 1), g, :].bitcast(F32), part[GR * g:GR * (g + 1), :].bitcast(F32)
                                     ).then_inc(stk_in, 16)
            experts(1)
            sp.wait_ge(mixed, 2 * NT)
            sp.dma_start(out_t, xres[:]).then_inc(stored, 16)
            sp.wait_ge(stored, 16)

        @block.gpsimd
        def _(pool):
            pool.memset(zero_rows[:], 0.0).then_inc(zeroed, 1)
            for ring, free in ((scan_done, 2), (read_ready, HD), (out_ready, 2), (oT_ready, 2), (krep_used, 1),
                               (update_ready, 1), (h_mm, 2 * NF), (ye_mm, 2), (h_ready, 2), (xeT_ready, 1),
                               (ye_ready, 1), (ye_out[0], 16), (ye_out[1], 16), (qf_ready, 2), (at_mm, 2),
                               (at_ready, 1), (xres_b, 1)):
                pool.sem_inc(ring, free)
            pool.memset(ident[:], 0.0)
            pool.memset(before_bf[:], -1.0)
            pool.memset(sel_f[:], 0.0)
            pool.memset(headsum[:], 1.0)
            pool.memset(ones_bf[:], 1.0)
            pool.memset(ones_row[:], 1.0)
            pool.memset(eps_col[:], EPS)
            pool.memset(first_tile[:], 1.0)
            for e in range(NE):
                pool.memset(expert_base[:, e, :], float(CAP * e))
                pool.memset(low_first[:, :, e], float(NE - e))
            pool.memset(minus_one[:], -1.0).then_inc(const_made, 1)
            pool.wait_ge(const_made, 1)
            pool.affine_select(out=ident[:], in_=ident[:], compare_op=ALU.not_equal, fill=1.0, base=0,
                               pattern=[[-1, P]], channel_multiplier=1).then_inc(const_made, 1)
            pool.affine_select(out=before_bf[:], in_=before_bf[:], compare_op=ALU.is_ge, fill=0.0, base=0,
                               pattern=[[-1, P]], channel_multiplier=1).then_inc(const_made, 1)
            pool.affine_select(out=sel_f[:].rearrange("p i (h j) -> p i h j", j=HD),
                               in_=sel_f[:].rearrange("p i (h j) -> p i h j", j=HD),
                               compare_op=ALU.not_equal, fill=1.0, base=0,
                               pattern=[[-1, HD], [-HD, H], [0, HD]], channel_multiplier=1).then_inc(sel_made, 1)
            pool.affine_select(out=headsum[:], in_=headsum[:], compare_op=ALU.is_ge, fill=0.0, base=0,
                               pattern=[[-HD, 32]], channel_multiplier=1).then_inc(const_made, 1)
            pool.wait_ge(const_made, 4)
            pool.affine_select(out=headsum[:], in_=headsum[:], compare_op=ALU.is_ge, fill=0.0, base=HD - 1,
                               pattern=[[HD, 32]], channel_multiplier=-1)
            pool.memset(first_tile[:, :, 0:1], 0.0).then_inc(const_made, 1)

            for c in range(NCH):
                for i in range(HD):
                    pool.wait_ge(scan_done, c * HD + i + 3)
                    pool.wait_ge(out_ready, c * 2 + i // 4 + 1)
                    pool.tensor_tensor(read[:, i, :], state[:, i, :], qT[:, c * CH:(c + 1) * CH],
                                       ALU.mult).then_inc(read_ready, 1)

            def experts(k):
                pool.wait_ge(index_ready, 2 * k + 1)
                pool.wait_ge(slots_clear, 16 * NE)
                for j in range(KT):
                    pool.indirect_dma_start(
                        out=slots_x, out_offset=bass.IndirectOffsetOnAxis(ap=put_at[:, j:j + 1], axis=0),
                        in_=xn[:, j % NT, :], in_offset=None, bounds_check=NE * CAP - 1, oob_is_err=False,
                    ).then_inc(scattered, 16)
                pool.wait_ge(index_ready, 2 * k + 2)
                for b in range(2):
                    pool.wait_ge(ye_out[b], 16 * (NE // 2) * (k + 1) + 16)
                for t in range(NT):
                    for kk in range(2):
                        j = kk * NT + t
                        pool.indirect_dma_start(
                            out=got[:, j, :], out_offset=None, in_=slots_y,
                            in_offset=bass.IndirectOffsetOnAxis(ap=get_at[:, j:j + 1], axis=0),
                        ).then_inc(gathered[t], 16)

            experts(0)
            pool.wait_ge(mixed, NT)
            pool.memset(projf[:], 0.0).then_inc(zeroed, 1)
            pool.memset(vaug[:, :, :, GR:GR + 1], 1.0)
            pool.memset(kvl[:], 0.0).then_inc(ones_made, 1)
            for n, stk in enumerate((pstk, kstk, qstk)):
                pool.wait_ge(ones_made, n + 1)
                pool.memset(stk[3 * GR:STK, :, :].bitcast(F32), 1.0).then_inc(ones_made, 1)
            experts(1)

        @block.scalar
        def _(act):
            copy = lambda o, i: act.activation(o, i, ACT.Copy)

            def layer_norm(n):
                act.wait_ge(ln_mv, NT * (n + 1))
                act.activation(std[:], mv[:, :, 1], ACT.Sqrt, bias=eps_col[:]).then_inc(ln_std, 1)

            def turned(n):
                for c in range(NB):
                    act.wait_ge(xn_turned, NB * n + c + 1)
                    copy(xnT[:, c * BK:(c + 1) * BK], ps[:, c, :]).then_inc(xnT_ready, 1)

            act.wait_ge(const_made, N_CONST)
            layer_norm(0)
            act.wait_ge(wT_mm, 1)
            for n, w in enumerate((wqT, wkT, wvT, woT)):
                copy(w[:], ps[:, 4, n * D:(n + 1) * D]).then_inc(wT_ready, 1)
            turned(0)

            for c in range(NB):
                for t in range(TB * c, TB * c + TB):
                    act.wait_ge(qkv_mm, t + 1)
                    copy(raw[:, t, :], ps[:, 4 + t % 4, 0:QKVB]).then_inc(raw_ready, 1)
                act.wait_ge(raw_ready, TB * (c + 1))
                act.activation(squares[:, TB * c:TB * c + TB, :], raw[:, TB * c:TB * c + TB, 0:2 * D],
                               ACT.Square).then_inc(sq_ready, 1)
            for c in range(NB):
                act.wait_ge(sumsq, c + 1)
                act.activation(rnorm[:, TB * c:TB * c + TB, :], norm[:, TB * c:TB * c + TB, :],
                               ACT.Sqrt).then_inc(norm_ready, 1)
            act.activation(beta[:], raw[:, :, 3 * D:QKVB], ACT.Sigmoid).then_inc(beta_ready, 1)

            for c in range(NB):
                for n, dst in enumerate((khi, vhi, qT, bkT)):
                    act.wait_ge(qkv_turned, 4 * c + n + 1)
                    copy(dst[:, c * BK:(c + 1) * BK], ps[:, 4 * (c % 2) + n, :]).then_inc(hi_ready, 1)

            with act.Fori(0, NCH) as c:
                for i in range(HD):
                    act.wait_ge(krep_used, c * HD + i + 2)
                    act.activation(decay[:, i % 2, :], decay[:, i % 2, :], ACT.Identity, scale=-1.0,
                                   bias=1.0).then_inc(decay_ready, 1)
                for ib in range(2):
                    act.wait_ge(out_ready, c * 2 + ib + 3)
                    copy(oT[:, ib, bass.ds(c * CH, CH)],
                         flat(ps[:, 4 + 2 * ib:6 + 2 * ib, :])).then_inc(oT_ready, 1)

            act.wait_ge(read_ready, HD + HD * NCH)
            for c in range(NB):
                act.wait_ge(gate_mm, c + 1)
                act.activation(qT[:, c * BK:(c + 1) * BK], ps[:, 4 + c, :], ACT.Silu).then_inc(gate_ready, 1)
            for c in range(2 * NB):
                act.wait_ge(o_turned, c + 1)
                copy(otok[:, 2 * c:2 * c + 2, :].rearrange("p t (h i) -> p t h i", i=HD),
                     ps[:, c % 4, :].rearrange("p (t i h) -> p t h i", t=2, i=HD)[:, :, 0:H, :]
                     ).then_inc(otok_ready, 1)
            layer_norm(1)
            for c in range(NB):
                act.wait_ge(xn_turned, NB + c + 1)
                act.activation(bkT[:, c * BK:(c + 1) * BK], ps[:, c, :], ACT.Identity, scale=lng[:],
                               bias=lnb[:]).then_inc(nT_ready, 1)

            def experts(k, n):
                layer_norm(n)
                turned(n)
                act.wait_ge(gap_ready, k + 1)
                act.activation(prob[:, 0:NT], gap[:], ACT.Sigmoid).then_inc(prob_ready, 1)
                act.activation(prob[:, NT:KT], gap[:], ACT.Sigmoid, scale=-1.0).then_inc(prob_ready, 1)
                act.wait_ge(cfc_in, 16 * (k + 1))
                with act.Fori(0, NE // 2) as pair:
                    for b in range(2):
                        e = pair * 2
                        s = k * NE + e + b
                        act.wait_ge(h_mm, s * NF + NF)
                        copy(wfc[:, b, :], flat(cfc_sb[:, bass.ds(e + b, 1), :])).then_inc(wfc_ready, 1)
                        act.wait_ge(xe_turned, s + 1)
                        copy(xeT[:, b, :], flat(ps[:, 0:2, :])[:, 0:CAP]).then_inc(xeT_ready, 1)
                        for f in range(NF):
                            act.wait_ge(h_mm, s * NF + f + 1 + 2 * NF)
                            if f == 0:
                                act.wait_ge(ye_mm, s + 1)
                            act.activation(hT[:, b, f, :].rearrange("p (a n) -> p a n", a=2),
                                           ps[:, 2 + 2 * (f % 2):4 + 2 * (f % 2), 0:HALF],
                                           ACT.Gelu).then_inc(h_ready, 1)

            experts(0, 2)

            layer_norm(3)
            turned(3)
            for c in range(NB):
                act.wait_ge(qkv2_mm, c + 1)
                if c == 0:
                    act.wait_ge(ones_made, 1)
                copy(vaug[:, TB * c:TB * c + TB, :, 0:GR],
                     ps[:, 4 + c, :].rearrange("p (t g r) -> p t g r", t=TB, g=NG)).then_inc(v2_ready, 1)
            act.wait_ge(proj_in, 16 * 3 * GH)
            copy(flat(pstk[0:3 * GR, :, :]), flat(projf[:])).then_inc(pstk_ready, 1)
            for n in range(2):
                if n:
                    act.wait_ge(stk_in, 16 * 3 * NG)
                for c in range(NB):
                    act.wait_ge(qkv2_mm, NB * (n + 1) + c + 1)
                    copy(part_hi[:, c * BK:(c + 1) * BK], ps[:, 4 * n + c, :]).then_inc(part_ready, 1)
            for s in range(2 * NT):
                act.wait_ge(kf_mm, s + 1)
                if s >= 3:
                    act.wait_ge(kf_ready, s - 2)
                act.activation(expo[:, s % 3, :], flat(ps[:, 2 * (s % 3):2 * (s % 3) + 2, :]), ACT.Exp,
                               bias=minus_one[:]).then_inc(kf_exp, 1)
            act.wait_ge(kv_mm, 2 * NT)
            for gm in range(2):
                rows = slice(64 * gm, 64 * gm + GR + 1)
                copy(kv_sb[rows, :, :], ps[rows, 6:8, :]).then_inc(kv_copied, 1)
            act.wait_ge(kf_ready, 2 * NT)
            with act.Fori(0, NB) as c:
                for j in range(8):
                    act.wait_ge(qf_mm, c * 8 + j + 1)
                    act.wait_ge(qf_ready, c * 8 + j + 1)
                    act.activation(expo[:, j % 2, :], flat(ps[:, 2 * (j % 2):2 * (j % 2) + 2, :]), ACT.Exp,
                                   bias=minus_one[:]).then_inc(qf_exp, 1)
                act.wait_ge(at_mm, c * 8 + 10)
                copy(flat(at_sb[:]), flat(ps[:, 4:6, :])).then_inc(at_ready, 1)
                act.wait_ge(att_turned, c + 1)
                copy(attT[:], ps[:, 6, :]).then_inc(attT_ready, 1)
            experts(1, 4)

        @block.vector
        def _(dve):
            def layer_norm(n, src, dst):
                for t in range(NT):
                    if n == 0 and t % TB == 0:
                        dve.wait_ge(x_in[t // TB], 16)
                    if n == 1 and t % 2 == 0:
                        dve.wait_ge(otok_ready, t // 2 + 1)
                    dve.bn_stats(stats[:, t, :], src[:, t, :]).then_inc(ln_stat, 1)
                for t in range(NT):
                    dve.wait_ge(ln_stat, NT * n + t + 1)
                    dve.bn_aggr(mv[:, t, :], stats[:, t, :]).then_inc(ln_mv, 1)
                dve.wait_ge(ln_std, n + 1)
                dve.reciprocal(rstd[:], std[:]).then_inc(ln_rstd, 1)
                dve.wait_ge(ln_rstd, n + 1)
                for t in range(NT):
                    dve.tensor_scalar(dst[:, t, :], src[:, t, :], mv[:, t, 0:1], rstd[:, t:t + 1],
                                      ALU.subtract, ALU.mult).then_inc(ln_out, 1)

            layer_norm(0, xres, xn)
            dve.wait_ge(sel_made, 1)
            dve.tensor_copy(sel[:], sel_f[:]).then_inc(sel_made, 1)

            for c in range(NB):
                dve.wait_ge(sq_ready, c + 1)
                dve.reduce_sum(norm[:, TB * c:TB * c + TB, :],
                               squares[:, TB * c:TB * c + TB, :].rearrange("p t (g d) -> p t g d", d=HD),
                               AX_X).then_inc(sumsq, 1)
            for c in range(NB):
                tt = slice(TB * c, TB * c + TB)
                dve.wait_ge(norm_ready, c + 1)
                dve.tensor_scalar(rnorm[:, tt, :], rnorm[:, tt, :], 1e-12, None, ALU.max).then_inc(rn_clamped, 1)
                dve.wait_ge(rn_clamped, c + 1)
                dve.reciprocal(rnorm[:, tt, :], rnorm[:, tt, :]).then_inc(rn_ready, 1)
                dve.wait_ge(rn_ready, c + 1)
                qk = raw[:, tt, 0:2 * D].rearrange("p t (g d) -> p t g d", d=HD)
                dve.tensor_tensor(qk, qk, rnorm[:, tt, :].unsqueeze(3).broadcast_to((P, TB, 2 * H, HD)),
                                  ALU.mult).then_inc(unit_ready, 1)
            dve.wait_ge(beta_ready, 1)
            for c in range(NB):
                tt = slice(TB * c, TB * c + TB)
                dve.wait_ge(unit_ready, c + 1)
                dve.tensor_tensor(bk[:, tt, :].rearrange("p t (h d) -> p t h d", d=HD),
                                  raw[:, tt, D:2 * D].rearrange("p t (h d) -> p t h d", d=HD),
                                  beta[:, tt, :].unsqueeze(3).broadcast_to((P, TB, H, HD)),
                                  ALU.mult).then_inc(bk_ready, 1)
            for c in range(NB):
                cc = slice(c * BK, (c + 1) * BK)
                for n, (hi, lo) in enumerate(((khi, klo), (vhi, vlo))):
                    dve.wait_ge(hi_ready, 4 * c + n + 1)
                    dve.tensor_tensor(lo[:, cc], ps[:, 4 * (c % 2) + n, :], hi[:, cc].bitcast(F32),
                                      ALU.subtract).then_inc(lo_ready, 1)

            dve.wait_ge(qkv_turned, 4 * NB)
            dve.memset(state[:, :, CH - 1:CH], 0.0).then_inc(carry_zero, 1)
            dve.wait_ge(carry_zero, 1)

            def scan(c, i):
                dve.wait_ge(decay_ready, c * HD + i + 1)
                dve.wait_ge(update_ready, c * HD + i + 2)
                dve.wait_ge(read_ready, c * HD + i + 1)
                dve.tensor_tensor_scan(out=state[:, i, :], data0=decay[:, i % 2, :], data1=update[:, i % 2, :],
                                       initial=state[:, i, CH - 1:CH], op0=ALU.mult,
                                       op1=ALU.add).then_inc(scan_done, 1)

            with dve.Fori(0, NCH) as c:
                for i in range(HD):
                    dve.wait_ge(krep_ready, c * HD + i + 1)
                    dve.wait_ge(scan_done, c * HD + i + 1)
                    dve.tensor_tensor(decay[:, i % 2, :], flat(ps[:, 0:2, :]), bkT[:, bass.ds(c * CH, CH)],
                                      ALU.mult).then_inc(krep_used, 1)
                    dve.wait_ge(vrep_ready, c * HD + i + 1)
                    dve.tensor_tensor(update[:, i % 2, :], flat(ps[:, 2:4, :]), bkT[:, bass.ds(c * CH, CH)],
                                      ALU.mult).then_inc(update_ready, 1)
                    if i:
                        scan(c, i - 1)
                scan(c, HD - 1)

            layer_norm(1, otok, otok)
            for c in range(NB):
                cc = slice(c * BK, (c + 1) * BK)
                dve.wait_ge(nT_ready, c + 1)
                dve.wait_ge(gate_ready, c + 1)
                dve.tensor_tensor(gated[:, cc], bkT[:, cc], qT[:, cc], ALU.mult).then_inc(gated_ready, 1)
            for c in range(NB):
                dve.wait_ge(y_mm, c + 1)
                rows = flat(xres[:, TB * c:TB * c + TB, :])
                dve.tensor_tensor(rows, ps[:, 4 + c, :], rows, ALU.add).then_inc(xres_a, 1)

            def experts(k, n):
                if k == 0:
                    dve.wait_ge(xres_a, NB)
                else:
                    dve.wait_ge(xres_b, NB + 1)
                    dve.wait_ge(scattered, 16 * KT)
                layer_norm(n, xres, xn)
                def link(ins):
                    steps[0] += 1
                    ins.then_inc(route_step, 1)
                    dve.wait_ge(route_step, steps[0])

                dve.wait_ge(logit_mm, k + 1)
                dve.tensor_copy(flat(lg[:]), ps[:, 4, 0:NT * NE]).then_inc(logit_ready, 1)
                dve.wait_ge(logit_ready, k + 1)
                by_choice = lambda c: chosen[:, :, c * NT:(c + 1) * NT].rearrange("p e t -> p t e")
                wide = lambda ap: ap.unsqueeze(2).broadcast_to((P, NT, NE))
                over_e = lambda t: t[:].rearrange("p e t -> p t e")
                for c, src in enumerate((lg, lg2)):
                    link(dve.tensor_reduce(top[:, c, :], src[:], AX_X, ALU.max))
                    link(dve.tensor_tensor(ranked[:], src[:], wide(top[:, c, :]), ALU.is_equal))
                    link(dve.tensor_tensor(ranked[:], ranked[:], low_first[:], ALU.mult))
                    link(dve.tensor_reduce(best[:, c, :], ranked[:], AX_X, ALU.max))
                    link(dve.tensor_tensor(by_choice(c), ranked[:], wide(best[:, c, :]), ALU.is_equal))
                    if c == 0:
                        link(dve.scalar_tensor_tensor(out=lg2[:], in0=by_choice(0), scalar=-1e30, in1=lg[:],
                                                      op0=ALU.mult, op1=ALU.add))
                dve.tensor_copy(chosen_bf[:], flat(chosen[:])).then_inc(chosen_ready, 1)
                dve.tensor_tensor(gap[:], top[:, 0, :], top[:, 1, :], ALU.subtract).then_inc(gap_ready, 1)
                link(dve.tensor_tensor(table2[:], chosen[:], expert_base[:], ALU.mult))
                link(dve.tensor_reduce(base[:], over_e(table2), AX_X, ALU.add))
                dve.wait_ge(count_mm, k + 1)
                link(dve.tensor_tensor_scan(out=upto[:], data0=flat(first_tile[:]), data1=ps[:, 5, 0:NE * KT],
                                            initial=0.0, op0=ALU.mult, op1=ALU.add))
                link(dve.tensor_tensor(flat(table[:]), ps[:, 5, NE * KT:2 * NE * KT], upto[:], ALU.add))
                link(dve.tensor_tensor(table[:], table[:], chosen[:], ALU.mult))
                link(dve.tensor_reduce(rank[:], over_e(table), AX_X, ALU.add))
                link(dve.tensor_single_scalar(kept[:], rank[:], float(CAP), ALU.is_lt))
                link(dve.tensor_tensor(slot[:], rank[:], base[:], ALU.add))
                link(dve.scalar_tensor_tensor(out=slot2[:], in0=kept[:], scalar=-FAR, in1=slot[:],
                                              op0=ALU.mult, op1=ALU.add))
                dve.tensor_scalar(put_at[:], slot2[:], FAR, None, ALU.add).then_inc(index_ready, 1)
                dve.tensor_scalar(get_at[:], slot2[:], FAR, float(NE * CAP - 1), ALU.add,
                                  ALU.min).then_inc(index_ready, 1)
                dve.wait_ge(prob_ready, 2 * k + 2)
                dve.tensor_tensor(weight[:], prob[:], kept[:], ALU.mult).then_inc(weight_ready, 1)

                with dve.Fori(0, NE // 2) as pair:
                    for b in range(2):
                        e = pair * 2
                        s = k * NE + e + b
                        dve.wait_ge(ye_mm, s + 3)
                        dve.wait_ge(ye_out[b], 16 * (NE // 2) * k + e * 8 + 16)
                        dve.tensor_copy(ye[:, b, :], flat(ps[:, 6:8, :])[:, 0:NS * D]).then_inc(ye_ready, 1)

                dve.wait_ge(weight_ready, k + 1)

                def second(t):
                    dve.wait_ge(mix_first, k * NT + t + 1)
                    dve.scalar_tensor_tensor(out=xres[:, t, :], in0=got[:, NT + t, :],
                                             scalar=weight[:, NT + t:NT + t + 1], in1=xres[:, t, :],
                                             op0=ALU.mult, op1=ALU.add).then_inc(mixed, 1)

                for t in range(NT):
                    dve.wait_ge(gathered[t], 32 * (k + 1))
                    dve.scalar_tensor_tensor(out=xres[:, t, :], in0=got[:, t, :], scalar=weight[:, t:t + 1],
                                             in1=xres[:, t, :], op0=ALU.mult, op1=ALU.add).then_inc(mix_first, 1)
                    if t:
                        second(t - 1)
                second(NT - 1)

            steps = [0]
            experts(0, 2)

            dve.wait_ge(mixed, NT)
            dve.wait_ge(scattered, 16 * KT)
            layer_norm(3, xres, xn)
            dve.wait_ge(pstk_ready, 1)
            lo = slice(2 * GR, 3 * GR)
            dve.tensor_tensor(flat(pstk[lo, :, :]), flat(projf[lo, :, :]), flat(pstk[lo, :, :]).bitcast(F32),
                              ALU.subtract).then_inc(pstklo_ready, 1)
            for n in range(2):
                if n:
                    dve.wait_ge(stk_in, 16 * 3 * NG)
                for c in range(NB):
                    cc = slice(c * BK, (c + 1) * BK)
                    dve.wait_ge(part_ready, NB * n + c + 1)
                    dve.tensor_tensor(part_lo[:, cc], ps[:, 4 * n + c, :], part_hi[:, cc].bitcast(F32),
                                      ALU.subtract).then_inc(partlo_ready, 1)
            for s in range(2 * NT):
                dve.wait_ge(kf_exp, s + 1)
                if s >= 3:
                    dve.wait_ge(kv_mm, s - 2)
                dve.scalar_tensor_tensor(out=feat[:, s % 3, :], in0=expo[:, s % 3, :], scalar=1.0,
                                         in1=flat(ps[:, 2 * (s % 3):2 * (s % 3) + 2, :]), op0=ALU.min,
                                         op1=ALU.max).then_inc(kf_ready, 1)
            dve.wait_ge(kv_turned, 1)
            dve.wait_ge(ones_made, 1)
            heads = ps[:, 4:6, :].rearrange("p m (q a c) -> p q m a c", q=2, a=GH)
            kvl_v = kvl[:].rearrange("p (q m a) c -> p q m a c", q=2, m=2)
            for a_ in range(GH):
                cols = slice(HD * a_, HD * (a_ + 1))
                dve.tensor_copy(kvl_v[:, :, :, a_, cols], heads[:, :, :, a_, cols]).then_inc(kvl_ready, 1)
                dve.tensor_copy(kvl_v[:, :, :, a_, GR + a_:GR + a_ + 1],
                                heads[:, :, :, a_, GR:GR + 1]).then_inc(kvl_ready, 1)
            dve.wait_ge(kv_mm, 2 * NT)
            with dve.Fori(0, NB) as c:
                for j in range(8):
                    dve.wait_ge(qf_exp, c * 8 + j + 1)
                    dve.wait_ge(at_mm, c * 8 + j + 1)
                    dve.scalar_tensor_tensor(out=feat[:, j % 2, :], in0=expo[:, j % 2, :], scalar=1.0,
                                             in1=flat(ps[:, 2 * (j % 2):2 * (j % 2) + 2, :]), op0=ALU.min,
                                             op1=ALU.max).then_inc(qf_ready, 1)
                dve.wait_ge(at_turned, c + 1)
                by_tok = flat(ps[:, 6:8, :]).rearrange("p (t g r) -> p t g r", t=TB, g=NG)
                dve.tensor_scalar(den[:].rearrange("p t (g a) -> p t g a", g=NG),
                                  by_tok[:, :, :, GR:GR + GH], 1e-8, None, ALU.add).then_inc(den_ready, 1)
                dve.wait_ge(den_ready, c + 1)
                dve.reciprocal(rden[:], den[:]).then_inc(rden_ready, 1)
                dve.wait_ge(rden_ready, c + 1)
                for t in range(TB):
                    dve.tensor_tensor(
                        att[:, t, :].rearrange("p (g a d) -> p g a d", g=NG, a=GH),
                        by_tok[:, t, :, 0:GR].rearrange("p g (a d) -> p g a d", a=GH),
                        rden[:, t, :].rearrange("p (g a) -> p g a", g=NG).unsqueeze(3).broadcast_to(
                            (P, NG, GH, HD)), ALU.mult).then_inc(att_ready, 1)
                dve.wait_ge(o2_mm, c + 1)
                rows = flat(xres[:, bass.ds(c * TB, TB), :])
                dve.tensor_tensor(rows, ps[:, 7, :], rows, ALU.add).then_inc(xres_b, 1)

            experts(1, 4)

        @block.tensor
        def _(pe):
            def mm(o, lhsT, rhs, start=True, stop=True, **kw):
                return pe.matmul(o, lhsT, rhs, start=start, stop=stop, **kw)

            def turn(n, base):
                src = otok if n == 1 else xn
                for t in range(NT):
                    pe.wait_ge(ln_out, NT * base + t + 1)
                    ins = pe.transpose(ps[:, t // TB, (t % TB) * P:(t % TB + 1) * P], src[:, t, :], ident[:])
                    if t % TB == TB - 1:
                        ins.then_inc(xn_turned, 1)

            pe.wait_ge(const_made, N_CONST)
            pe.wait_ge(wnat_in, 32)
            for n in range(4):
                ins = pe.transpose(ps[:, 4, n * D:(n + 1) * D], wnat[:, n, :], ident[:])
            ins.then_inc(wT_mm, 1)
            turn(0, 0)
            pe.wait_ge(w_in, 16 * 10)
            pe.wait_ge(wT_ready, 4)
            for t in range(NT):
                pe.wait_ge(xnT_ready, t // TB + 1)
                if t >= 4:
                    pe.wait_ge(raw_ready, t - 3)
                mm(ps[:, 4 + t % 4, 0:QKVB], xnT[:, t * P:(t + 1) * P], wall[:]).then_inc(qkv_mm, 1)
            pe.wait_ge(raw_ready, NT)
            for c in range(NB):
                pe.wait_ge(bk_ready, c + 1)
                if c >= 2:
                    pe.wait_ge(hi_ready, 4 * (c - 1))
                    pe.wait_ge(lo_ready, 2 * (c - 1))
                for n in range(4):
                    for t in range(TB):
                        tile = TB * c + t
                        src = (raw[:, tile, D:2 * D], raw[:, tile, 2 * D:3 * D], raw[:, tile, 0:D], bk[:, tile, :])[n]
                        ins = pe.transpose(ps[:, 4 * (c % 2) + n, t * P:(t + 1) * P], src, ident[:])
                    ins.then_inc(qkv_turned, 1)

            pe.wait_ge(hi_ready, 4 * NB)
            pe.wait_ge(lo_ready, 2 * NB)
            pe.wait_ge(sel_made, 2)

            def repeat(c, i, bank, hi, lo, done):
                for h in range(2):
                    cols = bass.ds(c * CH + h * BK, BK)
                    mm(ps[:, bank + h, :], sel[:, i, :], hi[:, cols], stop=False)
                    ins = mm(ps[:, bank + h, :], sel[:, i, :], lo[:, cols], start=False)
                ins.then_inc(done, 1)

            def sum_rows(c, ib):
                pe.wait_ge(read_ready, c * HD + HD + 4 * ib + 4)
                pe.wait_ge(oT_ready, c * 2 + ib + 1)
                for h in range(2):
                    for im in range(4):
                        ins = mm(ps[32 * im:32 * im + 32, 4 + 2 * ib + h, :], headsum[:],
                                 read[:, 4 * ib + im, h * BK:(h + 1) * BK], tile_position=(0, 32 * im))
                ins.then_inc(out_ready, 1)

            with pe.Fori(0, NCH) as c:
                for i in range(HD):
                    pe.wait_ge(krep_used, c * HD + i + 1)
                    repeat(c, i, 0, khi, klo, krep_ready)
                    pe.wait_ge(update_ready, c * HD + i + 1)
                    repeat(c, i, 2, vhi, vlo, vrep_ready)
                    if i == 6:
                        sum_rows(c, 0)
                sum_rows(c, 1)

            pe.wait_ge(oT_ready, 2 + 2 * NCH)
            for c in range(NB):
                mm(ps[:, 4 + c, :], wgate[:], xnT[:, c * BK:(c + 1) * BK]).then_inc(gate_mm, 1)
            pe.wait_ge(krep_used, HD * NCH + 1)
            pe.wait_ge(update_ready, HD * NCH + 1)
            for c in range(2 * NB):
                if c >= 4:
                    pe.wait_ge(otok_ready, c - 3)
                for t in range(2):
                    for ib in range(2):
                        col = (2 * t + ib) * P
                        ins = pe.transpose(ps[:, c % 4, col:col + P],
                                           oT[:, ib, (2 * c + t) * P:(2 * c + t + 1) * P], ident[:])
                ins.then_inc(o_turned, 1)
            pe.wait_ge(otok_ready, 2 * NB)
            turn(1, 1)
            pe.wait_ge(gate_ready, NB)
            for c in range(NB):
                pe.wait_ge(gated_ready, c + 1)
                for t in range(TB):
                    ins = mm(ps[:, 4 + c, t * P:(t + 1) * P], gated[:, (TB * c + t) * P:(TB * c + t + 1) * P], wout[:])
                ins.then_inc(y_mm, 1)

            def experts(k, n):
                turn(n, n)
                pe.wait_ge(ye_ready, k * NE + 1)
                for t in range(NT):
                    pe.wait_ge(xnT_ready, (n - 1 if n < 2 else n - 1) * NB + t // TB + 1)
                    ins = mm(ps[:, 4, t * NE:(t + 1) * NE], xnT[:, t * P:(t + 1) * P], wg_sb[:])
                ins.then_inc(logit_mm, 1)
                pe.wait_ge(chosen_ready, k + 1)
                mm(ps[:, 5, 0:NE * KT], ones_bf[:], chosen_bf[:])
                mm(ps[:, 5, NE * KT:2 * NE * KT], before_bf[:], chosen_bf[:]).then_inc(count_mm, 1)
                pe.wait_ge(cproj_in, 16)
                with pe.Fori(0, NE // 2) as pair:
                    for b in range(2):
                        e = pair * 2
                        s = k * NE + e + b
                        pe.wait_ge(xe_in[b], 16 * (NE // 2) * k + e * 8 + 16)
                        pe.wait_ge(xeT_ready, s + 1)
                        for i in range(NS):
                            ins = pe.transpose(ps[:, i // TB, (i % TB) * P:(i % TB + 1) * P], xe[:, b, i, :], ident[:])
                        ins.then_inc(xe_turned, 1)
                        pe.wait_ge(wfc_ready, s + 1)
                        pe.wait_ge(xeT_ready, s + 2)
                        for f in range(NF):
                            pe.wait_ge(h_ready, s * NF + f + 1)
                            for a_ in range(2):
                                ins = mm(ps[:, 2 + 2 * (f % 2) + a_, 0:HALF], wfc[:, b, f * P:(f + 1) * P],
                                         xeT[:, b, a_ * HALF:(a_ + 1) * HALF])
                            ins.then_inc(h_mm, 1)
                        pe.wait_ge(h_ready, s * NF + NF + 2)
                        pe.wait_ge(ye_ready, s + 1)
                        for i in range(NS):
                            for f in range(NF):
                                ins = mm(ps[:, 6 + i // TB, (i % TB) * P:(i % TB + 1) * P],
                                         hT[:, b, f, i * P:(i + 1) * P], cproj_sb[:, bass.ds(e + b, 1), f, :],
                                         start=f == 0, stop=f == NF - 1)
                        ins.then_inc(ye_mm, 1)

            experts(0, 2)

            turn(3, 3)
            for t in range(NT):
                pe.wait_ge(xnT_ready, 2 * NB + t // TB + 1)
                ins = mm(ps[:, 4 + t // TB, (t % TB) * P:(t % TB + 1) * P], xnT[:, t * P:(t + 1) * P], wvT[:])
                if t % TB == TB - 1:
                    ins.then_inc(qkv2_mm, 1)
            for c in range(NB):
                mm(ps[:, c, :], wkT[:], xnT[:, c * BK:(c + 1) * BK]).then_inc(qkv2_mm, 1)
            for c in range(NB):
                pe.wait_ge(v2_ready, c + 1)
                mm(ps[:, 4 + c, :], wqT[:], xnT[:, c * BK:(c + 1) * BK]).then_inc(qkv2_mm, 1)

            def key_features(s):
                t, gp = divmod(s, 2)
                if s >= 3:
                    pe.wait_ge(kf_ready, s - 2)
                for gm in range(2):
                    g = 2 * gp + gm
                    ins = mm(ps[:, 2 * (s % 3) + gm, :], kstk[:, g, t * P:(t + 1) * P], pstk[:, g, :])
                ins.then_inc(kf_mm, 1)

            pe.wait_ge(stk_in, 16 * 3 * NG)
            pe.wait_ge(ones_made, 4)
            pe.wait_ge(pstklo_ready, 1)
            pe.wait_ge(partlo_ready, 2 * NB)
            for s in range(3):
                key_features(s)
            for s in range(2 * NT):
                t, gp = divmod(s, 2)
                pe.wait_ge(kf_ready, s + 1)
                for gm in range(2):
                    ins = mm(ps[64 * gm:64 * gm + GR + 1, 6 + gp, :], vaug[:, t, 2 * gp + gm, :],
                             feat[:, s % 3, gm * BK:(gm + 1) * BK], start=t == 0, stop=t == NT - 1,
                             tile_position=(0, 64 * gm))
                ins.then_inc(kv_mm, 1)
                if s + 3 < 2 * NT:
                    key_features(s + 3)
            for gm in range(2):
                rows = slice(64 * gm, 64 * gm + GR + 1)
                pe.wait_ge(kv_copied, gm + 1)
                for n in range(2 * GH):
                    gp, a_ = divmod(n, GH)
                    ins = pe.transpose(ps[:, 4 + gm, n * 64:n * 64 + GR + 1],
                                       kv_sb[rows, gp, a_ * F:(a_ + 1) * F], ident[rows, rows])
            ins.then_inc(kv_turned, 1)

            def query_features(c, j):
                gp, a_ = divmod(j, GH)
                pe.wait_ge(qf_ready, c * 8 + j + 1)
                for gm in range(2):
                    g = 2 * gp + gm
                    ins = mm(ps[:, 2 * (j % 2) + gm, :], pstk[:, g, a_ * F:(a_ + 1) * F],
                             qstk[:, g, bass.ds(c * BK, BK)])
                ins.then_inc(qf_mm, 1)

            pe.wait_ge(stk_in, 2 * 16 * 3 * NG)
            pe.wait_ge(kvl_ready, 2 * GH)
            with pe.Fori(0, NB) as c:
                query_features(c, 0)
                query_features(c, 1)
                pe.wait_ge(at_ready, c + 1)
                for j in range(8):
                    gp, a_ = divmod(j, GH)
                    pe.wait_ge(qf_ready, c * 8 + j + 3)
                    for gm in range(2):
                        h = (2 * gp + gm) * GH + a_
                        ins = mm(ps[64 * gm:64 * gm + 64, 4 + gp, :], kvl[:, h, :],
                                 feat[:, j % 2, gm * BK:(gm + 1) * BK], start=a_ == 0, stop=a_ == GH - 1,
                                 tile_position=(0, 64 * gm))
                    ins.then_inc(at_mm, 1)
                    if j + 2 < 8:
                        query_features(c, j + 2)
                pe.wait_ge(at_ready, c + 2)
                pe.wait_ge(xres_b, c + 1)
                for t in range(TB):
                    for gp in range(2):
                        col = (2 * (t % 2) + gp) * P
                        ins = pe.transpose(ps[:, 6 + t // 2, col:col + P], at_sb[:, gp, t * P:(t + 1) * P], ident[:])
                ins.then_inc(at_turned, 1)
                pe.wait_ge(att_ready, c * TB + TB)
                for t in range(TB):
                    ins = pe.transpose(ps[:, 6, t * P:(t + 1) * P], att[:, t, :], ident[:])
                ins.then_inc(att_turned, 1)
                pe.wait_ge(attT_ready, c + 1)
                for t in range(TB):
                    mm(ps[:, 7, t * P:(t + 1) * P], attT[:, t * P:(t + 1) * P], woT[:], stop=False)
                    ins = mm(ps[:, 7, t * P:(t + 1) * P], ones_row[:], bout_row[:], start=False)
                ins.then_inc(o2_mm, 1)

            experts(1, 4)


_INS = ["L0_attn_a_x", "L0_attn_a_Wq", "L0_attn_a_Wk", "L0_attn_a_Wv", "L0_attn_a_Wbeta", "L0_attn_a_Wg",
        "L0_attn_a_Wout", "L0_attn_a_ln_g", "L0_attn_a_ln_b", "L0_attn_b_W_qkv", "L0_attn_b_proj",
        "L0_attn_b_W_out", "L0_attn_b_b_out", "L0_ffn_w_g", "L0_ffn_c_fc", "L0_ffn_c_proj"]


def kernel(**inputs):
    import numpy as np
    import concourse.bacc as bacc
    from concourse.bass_utils import run_bass_kernel_spmd

    nc = bacc.Bacc("TRN2", target_bir_lowering=False, num_devices=1)
    arrays, args = {}, []
    for name in _INS:
        a = np.ascontiguousarray(inputs[name])
        arrays["in_" + name] = a
        args.append(nc.dram_tensor("in_" + name, a.shape, mybir.dt.from_np(a.dtype), kind="ExternalInput").ap())
    out = nc.dram_tensor("out_0", (1, TOK, D), F32, kind="ExternalOutput").ap()
    program(nc, *args, out)
    r = run_bass_kernel_spmd(nc, [arrays], core_ids=[0])
    return r.results[0]["out_0"]
```

```python
from contextlib import ExitStack

import concourse.bass as bass
from concourse import mybir

F32 = mybir.dt.float32
F32R = mybir.dt.float32r
BF16 = mybir.dt.bfloat16
I32 = mybir.dt.int32
ALU = mybir.AluOpType
ACT = mybir.ActivationFunctionType
AX_X = mybir.AxisListType.X

P = 128
TOK = 2048
D = 128
NT = TOK // P
H = 16
HD = D // H
EPS = 1e-5
BK = 512
NB = TOK // BK
TB = BK // P

QKVB = 3 * D + H
CH = 1024
NCH = TOK // CH

NE = 8
FF = 4 * D
NF = FF // P
CAP = 640
NS = CAP // P
HALF = CAP // 2
KT = 2 * NT
ROW = D + 1
FAR = 65536.0

NG = 4
GH = H // NG
GR = GH * HD
STK = 3 * GR + 1
F = 128


def program(nc, x, Wq, Wk, Wv, Wbeta, Wg, Wout, ln_g, ln_b, W_qkv, proj, W_out, b_out, w_g, c_fc, c_proj, out):
    ctx = ExitStack()

    def sb(name, shape, dt=F32, stack=None):
        return (stack or ctx).enter_context(nc.sbuf_tensor(name, shape, dt))

    def sem(name):
        return ctx.enter_context(nc.semaphore(name))

    with ctx:
        ps = ctx.enter_context(nc.psum_tensor("ps", [P, 8, BK], F32))
        xres = sb("xres", [P, NT, D])
        xn = sb("xn", [P, NT, D])
        xnT = sb("xnT", [P, TOK])
        ident = sb("ident", [P, P])
        ones_bf = sb("ones_bf", [P, P], BF16)
        before_bf = sb("before_bf", [P, P], BF16)
        first_tile = sb("first_tile", [P, NE, KT])
        expert_base = sb("expert_base", [P, NE, KT])
        low_first = sb("low_first", [P, NT, NE])
        minus_one = sb("minus_one", [P, 1])
        eps_col = sb("eps_col", [P, 1])
        ones_row = sb("ones_row", [1, P])
        stats = sb("stats", [P, NT, 6])
        mv = sb("mv", [P, NT, 2])
        std = sb("std", [P, NT])
        rstd = sb("rstd", [P, NT])
        wg_sb = sb("wg_sb", [P, NE])
        cproj_sb = sb("cproj_sb", [P, NE, NF, D])
        bout_row = sb("bout_row", [1, D])
        empty_rows = sb("empty_rows", [P, NS, ROW])
        wvT = sb("wvT", [P, D])
        wkT = sb("wkT", [P, D])
        wqT = sb("wqT", [P, D])
        woT = sb("woT", [P, D])
        slots_x = [nc.dram_tensor(f"slots_x{k}", [NE * CAP, ROW], F32).ap() for k in range(2)]
        chosen_y = nc.dram_tensor("chosen_y", [KT * P, D], F32).ap()

        with ExitStack() as a:
            wall = sb("wall", [P, QKVB], F32, a)
            wgate = sb("wgate", [P, D], F32, a)
            wout = sb("wout", [P, D], F32, a)
            lng = sb("lng", [P, 1], F32, a)
            lnb = sb("lnb", [P, 1], F32, a)
            wnat = sb("wnat", [P, 4, D], F32, a)
            sel_f = sb("sel_f", [P, HD, P], F32, a)
            sel = sb("sel", [P, HD, P], F32R, a)
            headsum = sb("headsum", [P, 32], F32, a)
            qT = sb("qT", [P, TOK], F32, a)
            bkT = sb("bkT", [P, TOK], F32, a)
            with ExitStack() as a1:
                khi = sb("khi", [P, TOK], F32R, a1)
                klo = sb("klo", [P, TOK], F32R, a1)
                vhi = sb("vhi", [P, TOK], F32R, a1)
                vlo = sb("vlo", [P, TOK], F32R, a1)
                with ExitStack() as a2:
                    raw = sb("raw", [P, NT, QKVB], F32, a2)
                    squares = sb("squares", [P, NT, 2 * D], F32, a2)
                    norm = sb("norm", [P, NT, 2 * H], F32, a2)
                    rnorm = sb("rnorm", [P, NT, 2 * H], F32, a2)
                    beta = sb("beta", [P, NT, H], F32, a2)
                    bk = sb("bk", [P, NT, D], F32, a2)
                with ExitStack() as a3:
                    decay = sb("decay", [P, 2, CH], F32, a3)
                    update = sb("update", [P, 2, CH], F32, a3)
                    state = sb("state", [P, HD, CH], F32, a3)
                    read = sb("read", [P, HD, CH], F32, a3)
                    oT = sb("oT", [P, 2, TOK], F32, a3)
            with ExitStack() as a4:
                otok = sb("otok", [P, NT, D], F32, a4)
                gated = sb("gated", [P, TOK], F32, a4)

        with ExitStack() as m:
            cfc_sb = sb("cfc_sb", [P, NE, FF], F32, m)
            lg = sb("lg", [P, NT, NE], F32, m)
            lg2 = sb("lg2", [P, NT, NE], F32, m)
            ranked = sb("ranked", [P, NT, NE], F32, m)
            top = sb("top", [P, 2, NT], F32, m)
            best = sb("best", [P, 2, NT], F32, m)
            gap = sb("gap", [P, NT], F32, m)
            prob = sb("prob", [P, KT], F32, m)
            chosen = sb("chosen", [P, NE, KT], F32, m)
            chosen_bf = sb("chosen_bf", [P, NE * KT], BF16, m)
            upto = sb("upto", [P, NE * KT], F32, m)
            table = sb("table", [P, NE, KT], F32, m)
            table2 = sb("table2", [P, NE, KT], F32, m)
            rank = sb("rank", [P, KT], F32, m)
            base = sb("base", [P, KT], F32, m)
            kept = sb("kept", [P, KT], F32, m)
            slot = sb("slot", [P, KT], F32, m)
            slot2 = sb("slot2", [P, KT], F32, m)
            put_at = sb("put_at", [P, KT], I32, m)
            weight = sb("weight", [P, KT], F32, m)
            rows_x = sb("rows_x", [P, KT, ROW], F32, m)
            xe = sb("xe", [P, 2, NS, ROW], F32, m)
            y_to = sb("y_to", [P, 2, NS], I32, m)
            xeT = sb("xeT", [P, 2, CAP], F32, m)
            wfc = sb("wfc", [P, 2, FF], F32, m)
            hT = sb("hT", [P, 2, NF, CAP], F32, m)
            ye = sb("ye", [P, 2, NS * D], F32, m)
            got = sb("got", [P, KT, D], F32, m)

        with ExitStack() as b:
            projf = sb("projf", [3 * GR, NG, BK], F32, b)
            pstk = sb("pstk", [STK, NG, BK], F32R, b)
            kstk = sb("kstk", [STK, NG, TOK], F32R, b)
            qstk = sb("qstk", [STK, NG, TOK], F32R, b)
            part_hi = sb("part_hi", [P, TOK], F32R, b)
            part_lo = sb("part_lo", [P, TOK], F32R, b)
            vaug = sb("vaug", [P, NT, NG, GR + 1], F32, b)
            expo = sb("expo", [P, 3, 2 * BK], F32, b)
            feat = sb("feat", [P, 3, 2 * BK], F32, b)
            kv_sb = sb("kv_sb", [P, 2, BK], F32, b)
            kvl = sb("kvl", [P, H, 64], F32, b)
            at_sb = sb("at_sb", [P, 2, BK], F32, b)
            den = sb("den", [P, TB, H], F32, b)
            rden = sb("rden", [P, TB, H], F32, b)
            att = sb("att", [P, TB, D], F32, b)
            attT = sb("attT", [P, BK], F32, b)

        x_in = [sem(f"x_in{c}") for c in range(NB)]
        w_in = sem("w_in")
        wnat_in = sem("wnat_in")
        cproj_in = sem("cproj_in")
        cfc_in = sem("cfc_in")
        proj_in = sem("proj_in")
        zeroed = sem("zeroed")
        const_made = sem("const_made")
        sel_made = sem("sel_made")
        slots_clear, y_clear = sem("slots_clear"), sem("y_clear")
        ln_stat, ln_mv, ln_std, ln_rstd, ln_out = (sem(n) for n in ("ln_stat", "ln_mv", "ln_std", "ln_rstd", "ln_out"))
        xn_turned, xnT_ready = sem("xn_turned"), sem("xnT_ready")
        wT_mm, wT_ready = sem("wT_mm"), sem("wT_ready")
        qkv_mm, raw_ready, sq_ready, sumsq, norm_ready = (
            sem(n) for n in ("qkv_mm", "raw_ready", "sq_ready", "sumsq", "norm_ready"))
        rn_clamped, rn_ready, unit_ready, beta_ready, bk_ready = (
            sem(n) for n in ("rn_clamped", "rn_ready", "unit_ready", "beta_ready", "bk_ready"))
        qkv_turned, hi_ready, lo_ready = sem("qkv_turned"), sem("hi_ready"), sem("lo_ready")
        carry_zero = sem("carry_zero")
        krep_ready, krep_used, vrep_ready, update_ready = (
            sem(n) for n in ("krep_ready", "krep_used", "vrep_ready", "update_ready"))
        decay_ready, scan_done, read_ready, out_ready, oT_ready = (
            sem(n) for n in ("decay_ready", "scan_done", "read_ready", "out_ready", "oT_ready"))
        o_turned, otok_ready, gate_mm, gate_ready, nT_ready, gated_ready, y_mm = (
            sem(n) for n in ("o_turned", "otok_ready", "gate_mm", "gate_ready", "nT_ready", "gated_ready", "y_mm"))
        xres_a = sem("xres_a")
        logit_mm, logit_ready, route_step, prob_ready = (
            sem(n) for n in ("logit_mm", "logit_ready", "route_step", "prob_ready"))
        chosen_ready, count_mm, index_ready, weight_ready, scattered = (
            sem(n) for n in ("chosen_ready", "count_mm", "index_ready", "weight_ready", "scattered"))
        xe_in = [sem(f"xe_in{i}") for i in range(2)]
        ye_out = [sem(f"ye_out{i}") for i in range(2)]
        xe_turned, xeT_ready, wfc_ready, h_mm, h_ready, ye_mm, ye_ready = (
            sem(n) for n in ("xe_turned", "xeT_ready", "wfc_ready", "h_mm", "h_ready", "ye_mm", "ye_ready"))
        rows_made, y_to_ready = sem("rows_made"), sem("y_to_ready")
        got_in = [sem(f"got_in{c}") for c in range(NB)]
        mix_first = sem("mix_first")
        gap_ready, pstklo_ready = sem("gap_ready"), sem("pstklo_ready")
        mixed = sem("mixed")
        qkv2_mm, v2_ready, part_ready, partlo_ready, stk_in = (
            sem(n) for n in ("qkv2_mm", "v2_ready", "part_ready", "partlo_ready", "stk_in"))
        pstk_ready, ones_made = sem("pstk_ready"), sem("ones_made")
        kf_mm, kf_exp, kf_ready, kv_mm = (sem(n) for n in ("kf_mm", "kf_exp", "kf_ready", "kv_mm"))
        kv_copied, kv_turned, kvl_ready = sem("kv_copied"), sem("kv_turned"), sem("kvl_ready")
        qf_mm, qf_exp, qf_ready, at_mm = (sem(n) for n in ("qf_mm", "qf_exp", "qf_ready", "at_mm"))
        at_ready, at_turned, den_ready, rden_ready, att_ready, att_turned, attT_ready, o2_mm, xres_b = (
            sem(n) for n in ("at_ready", "at_turned", "den_ready", "rden_ready", "att_ready", "att_turned",
                             "attT_ready", "o2_mm", "xres_b"))
        stored = sem("stored")

        N_CONST = 5
        block = ctx.enter_context(nc.Block())
        x_t = x.rearrange("a (t p) d -> p (a t) d", p=P)
        out_t = out.rearrange("a (t p) d -> p (a t) d", p=P)
        flat = lambda ap: ap.rearrange("p a b -> p (a b)")

        @block.sync
        def _(sp):
            for c in range(NB):
                sp.dma_start(xres[:, TB * c:TB * c + TB, :], x_t[:, TB * c:TB * c + TB, :]).then_inc(x_in[c], 16)
            for n, w in enumerate((Wq, Wk, Wv)):
                sp.dma_start(wall[:, n * D:(n + 1) * D], w).then_inc(w_in, 16)
            sp.dma_start(wall[:, 3 * D:QKVB], Wbeta).then_inc(w_in, 16)
            sp.dma_start(wnat[:, 0:3, :], W_qkv.rearrange("(n p) d -> p n d", p=P)).then_inc(wnat_in, 16)
            sp.dma_start(wnat[:, 3, :], W_out).then_inc(wnat_in, 16)
            sp.dma_start(wgate[:], Wg).then_inc(w_in, 16)
            sp.dma_start(wout[:], Wout).then_inc(w_in, 16)
            sp.dma_start(lng[:], ln_g.rearrange("(p a) -> p a", a=1)).then_inc(w_in, 16)
            sp.dma_start(lnb[:], ln_b.rearrange("(p a) -> p a", a=1)).then_inc(w_in, 16)
            sp.dma_start(wg_sb[:], w_g).then_inc(w_in, 16)
            sp.dma_start(bout_row[:], b_out.rearrange("(a d) -> a d", a=1)).then_inc(w_in, 16)
            sp.dma_start(cproj_sb[:], c_proj.rearrange("e (c p) d -> p e c d", p=P)).then_inc(cproj_in, 16)
            sp.wait_ge(zeroed, 1)
            for k in range(2):
                for e in range(NE):
                    sp.dma_start(slots_x[k][e * CAP:(e + 1) * CAP, :].rearrange("(p s) d -> p (s d)", s=NS),
                                 flat(empty_rows[:])).then_inc(slots_clear, 16)
            for j in range(0, KT, 4):
                sp.dma_start(chosen_y[j * P:(j + 4) * P, :].rearrange("(j p) d -> p j d", p=P),
                             empty_rows[:, 0:4, 0:D]).then_inc(y_clear, 16)

            def experts(k):
                if k == 0:
                    sp.wait_ge(xres_a, NB)
                else:
                    sp.wait_ge(xres_b, NB + 1)
                sp.dma_start(cfc_sb[:], c_fc.rearrange("e d f -> d e f")).then_inc(cfc_in, 16)
                sp.wait_ge(scattered, 16 * KT * (k + 1))

                def load(e, b):
                    sp.dma_start(flat(xe[:, b, :, :]),
                                 slots_x[k][bass.ds(e * CAP, CAP), :].rearrange("(p s) d -> p (s d)", s=NS)
                                 ).then_inc(xe_in[b], 16)

                for b in range(2):
                    load(b, b)
                with sp.Fori(0, NE // 2 - 1) as pair:
                    for b in range(2):
                        e = pair * 2
                        sp.wait_ge(xe_turned, k * NE + e + b + 1)
                        sp.wait_ge(y_to_ready, k * NE + e + b + 1)
                        load(e + b + 2, b)
                for b in range(2):
                    sp.wait_ge(ye_out[b], 16 * NS * (NE // 2) * (k + 1))
                for c in range(NB):
                    for kk in range(2):
                        j = kk * NT + TB * c
                        sp.dma_start(got[:, j:j + TB, :],
                                     chosen_y[j * P:(j + TB) * P, :].rearrange("(j p) d -> p j d", p=P)
                                     ).then_inc(got_in[c], 16)

            experts(0)
            sp.wait_ge(mixed, NT)
            sp.wait_ge(zeroed, 2)
            for r in range(3):
                for a_ in range(GH):
                    row = GR * r + HD * a_
                    sp.dma_start(projf[row:row + HD, :, a_ * F:(a_ + 1) * F],
                                 proj.rearrange("(g a) d f -> a d g f", a=GH)[a_]).then_inc(proj_in, 16)
            for n, stk in enumerate((kstk, qstk)):
                sp.wait_ge(part_ready, NB * (n + 1))
                sp.wait_ge(partlo_ready, NB * (n + 1))
                for g in range(NG):
                    for r, part in enumerate((part_hi, part_lo, part_hi)):
                        sp.dma_start(stk[GR * r:GR * (r + 1), g, :].bitcast(F32), part[GR * g:GR * (g + 1), :].bitcast(F32)
                                     ).then_inc(stk_in, 16)
            experts(1)
            sp.wait_ge(mixed, 2 * NT)
            sp.dma_start(out_t, xres[:]).then_inc(stored, 16)
            sp.wait_ge(stored, 16)

        @block.gpsimd
        def _(pool):
            pool.memset(empty_rows[:, :, 0:D], 0.0)
            pool.memset(empty_rows[:, :, D:ROW].bitcast(I32), int(FAR)).then_inc(zeroed, 1)
            for ring, free in ((scan_done, 2), (read_ready, HD), (out_ready, 2), (oT_ready, 2), (krep_used, 1),
                               (update_ready, 1), (h_mm, 2 * NF), (ye_mm, 2), (h_ready, 2), (xeT_ready, 1),
                               (ye_ready, 1), (qf_ready, 4), (at_mm, 2),
                               (at_ready, 1), (xres_b, 1)):
                pool.sem_inc(ring, free)
            pool.memset(ident[:], 0.0)
            pool.memset(before_bf[:], -1.0)
            pool.memset(sel_f[:], 0.0)
            pool.memset(headsum[:], 1.0)
            pool.memset(ones_bf[:], 1.0)
            pool.memset(ones_row[:], 1.0)
            pool.memset(eps_col[:], EPS)
            pool.memset(first_tile[:], 1.0)
            for e in range(NE):
                pool.memset(expert_base[:, e, :], float(CAP * e))
                pool.memset(low_first[:, :, e], float(NE - e))
            pool.memset(minus_one[:], -1.0).then_inc(const_made, 1)
            pool.wait_ge(const_made, 1)
            pool.affine_select(out=ident[:], in_=ident[:], compare_op=ALU.not_equal, fill=1.0, base=0,
                               pattern=[[-1, P]], channel_multiplier=1).then_inc(const_made, 1)
            pool.affine_select(out=before_bf[:], in_=before_bf[:], compare_op=ALU.is_ge, fill=0.0, base=0,
                               pattern=[[-1, P]], channel_multiplier=1).then_inc(const_made, 1)
            pool.affine_select(out=sel_f[:].rearrange("p i (h j) -> p i h j", j=HD),
                               in_=sel_f[:].rearrange("p i (h j) -> p i h j", j=HD),
                               compare_op=ALU.not_equal, fill=1.0, base=0,
                               pattern=[[-1, HD], [-HD, H], [0, HD]], channel_multiplier=1).then_inc(sel_made, 1)
            pool.affine_select(out=headsum[:], in_=headsum[:], compare_op=ALU.is_ge, fill=0.0, base=0,
                               pattern=[[-HD, 32]], channel_multiplier=1).then_inc(const_made, 1)
            pool.wait_ge(const_made, 4)
            pool.affine_select(out=headsum[:], in_=headsum[:], compare_op=ALU.is_ge, fill=0.0, base=HD - 1,
                               pattern=[[HD, 32]], channel_multiplier=-1)
            pool.memset(first_tile[:, :, 0:1], 0.0).then_inc(const_made, 1)

            for c in range(NCH):
                for i in range(HD):
                    pool.wait_ge(scan_done, c * HD + i + 3)
                    pool.wait_ge(out_ready, c * 2 + i // 4 + 1)
                    pool.tensor_tensor(read[:, i, :], state[:, i, :], qT[:, c * CH:(c + 1) * CH],
                                       ALU.mult).then_inc(read_ready, 1)

            def experts(k):
                if k == 0:
                    pool.wait_ge(xres_a, NB)
                else:
                    pool.wait_ge(xres_b, NB + 1)
                pool.iota(rows_x[:, :, D].bitcast(I32), [[P, KT]], base=0, channel_multiplier=1).then_inc(rows_made, 1)
                pool.wait_ge(rows_made, 3 * (k + 1))
                pool.wait_ge(index_ready, k + 1)
                pool.wait_ge(slots_clear, 16 * NE * 2)
                for j in range(KT):
                    pool.indirect_dma_start(
                        out=slots_x[k], out_offset=bass.IndirectOffsetOnAxis(ap=put_at[:, j:j + 1], axis=0),
                        in_=rows_x[:, j, :], in_offset=None, bounds_check=NE * CAP - 1, oob_is_err=False,
                    ).then_inc(scattered, 16)
                pool.wait_ge(y_clear, 16 * KT // 4)
                for e in range(NE):
                    b = e % 2
                    pool.wait_ge(ye_ready, k * NE + e + 2)
                    for i in range(NS):
                        pool.indirect_dma_start(
                            out=chosen_y, out_offset=bass.IndirectOffsetOnAxis(ap=y_to[:, b, i:i + 1], axis=0),
                            in_=ye[:, b, i * D:(i + 1) * D], in_offset=None, bounds_check=KT * P - 1,
                            oob_is_err=False,
                        ).then_inc(ye_out[b], 16)

            experts(0)
            pool.wait_ge(mixed, NT)
            pool.memset(projf[:], 0.0).then_inc(zeroed, 1)
            pool.memset(vaug[:, :, :, GR:GR + 1], 1.0)
            pool.memset(kvl[:], 0.0).then_inc(ones_made, 1)
            for n, stk in enumerate((pstk, kstk, qstk)):
                pool.wait_ge(ones_made, n + 1)
                pool.memset(stk[3 * GR:STK, :, :].bitcast(F32), 1.0).then_inc(ones_made, 1)
            experts(1)

        @block.scalar
        def _(act):
            copy = lambda o, i: act.activation(o, i, ACT.Copy)

            def layer_norm(n):
                act.wait_ge(ln_mv, NT * (n + 1))
                act.activation(std[:], mv[:, :, 1], ACT.Sqrt, bias=eps_col[:]).then_inc(ln_std, 1)

            def turned(n):
                for c in range(NB):
                    act.wait_ge(xn_turned, NB * n + c + 1)
                    copy(xnT[:, c * BK:(c + 1) * BK], ps[:, c, :]).then_inc(xnT_ready, 1)

            act.wait_ge(const_made, N_CONST)
            layer_norm(0)
            act.wait_ge(wT_mm, 1)
            for n, w in enumerate((wqT, wkT, wvT, woT)):
                copy(w[:], ps[:, 4, n * D:(n + 1) * D]).then_inc(wT_ready, 1)
            turned(0)

            for c in range(NB):
                for t in range(TB * c, TB * c + TB):
                    act.wait_ge(qkv_mm, t + 1)
                    copy(raw[:, t, :], ps[:, 4 + t % 4, 0:QKVB]).then_inc(raw_ready, 1)
                act.wait_ge(raw_ready, TB * (c + 1))
                act.activation(squares[:, TB * c:TB * c + TB, :], raw[:, TB * c:TB * c + TB, 0:2 * D],
                               ACT.Square).then_inc(sq_ready, 1)
            for c in range(NB):
                act.wait_ge(sumsq, c + 1)
                act.activation(rnorm[:, TB * c:TB * c + TB, :], norm[:, TB * c:TB * c + TB, :],
                               ACT.Sqrt).then_inc(norm_ready, 1)
            act.activation(beta[:], raw[:, :, 3 * D:QKVB], ACT.Sigmoid).then_inc(beta_ready, 1)

            for c in range(NB):
                for n, dst in enumerate((khi, vhi, qT, bkT)):
                    act.wait_ge(qkv_turned, 4 * c + n + 1)
                    copy(dst[:, c * BK:(c + 1) * BK], ps[:, 4 * (c % 2) + n, :]).then_inc(hi_ready, 1)

            with act.Fori(0, NCH) as c:
                for i in range(HD):
                    act.wait_ge(krep_used, c * HD + i + 2)
                    act.activation(decay[:, i % 2, :], decay[:, i % 2, :], ACT.Identity, scale=-1.0,
                                   bias=1.0).then_inc(decay_ready, 1)
                for ib in range(2):
                    act.wait_ge(out_ready, c * 2 + ib + 3)
                    copy(oT[:, ib, bass.ds(c * CH, CH)],
                         flat(ps[:, 4 + 2 * ib:6 + 2 * ib, :])).then_inc(oT_ready, 1)

            act.wait_ge(read_ready, HD + HD * NCH)
            for c in range(NB):
                act.wait_ge(gate_mm, c + 1)
                act.activation(qT[:, c * BK:(c + 1) * BK], ps[:, 4 + c, :], ACT.Silu).then_inc(gate_ready, 1)
            for c in range(2 * NB):
                act.wait_ge(o_turned, c + 1)
                copy(otok[:, 2 * c:2 * c + 2, :].rearrange("p t (h i) -> p t h i", i=HD),
                     ps[:, c % 4, :].rearrange("p (t i h) -> p t h i", t=2, i=HD)[:, :, 0:H, :]
                     ).then_inc(otok_ready, 1)
            layer_norm(1)
            for c in range(NB):
                act.wait_ge(xn_turned, NB + c + 1)
                act.activation(bkT[:, c * BK:(c + 1) * BK], ps[:, c, :], ACT.Identity, scale=lng[:],
                               bias=lnb[:]).then_inc(nT_ready, 1)

            def experts(k, n):
                layer_norm(n)
                turned(n)
                act.wait_ge(ln_out, NT * (n + 1))
                for kk in range(2):
                    copy(rows_x[:, kk * NT:(kk + 1) * NT, 0:D], xn[:]).then_inc(rows_made, 1)
                act.wait_ge(gap_ready, k + 1)
                act.activation(prob[:, 0:NT], gap[:], ACT.Sigmoid).then_inc(prob_ready, 1)
                act.activation(prob[:, NT:KT], gap[:], ACT.Sigmoid, scale=-1.0).then_inc(prob_ready, 1)
                act.wait_ge(cfc_in, 16 * (k + 1))
                with act.Fori(0, NE // 2) as pair:
                    for b in range(2):
                        e = pair * 2
                        s = k * NE + e + b
                        act.wait_ge(h_mm, s * NF + NF)
                        copy(wfc[:, b, :], flat(cfc_sb[:, bass.ds(e + b, 1), :])).then_inc(wfc_ready, 1)
                        act.wait_ge(xe_turned, s + 1)
                        copy(xeT[:, b, :], flat(ps[:, 0:2, :])[:, 0:CAP]).then_inc(xeT_ready, 1)
                        for f in range(NF):
                            act.wait_ge(h_mm, s * NF + f + 1 + 2 * NF)
                            if f == 0:
                                act.wait_ge(ye_mm, s + 1)
                            act.activation(hT[:, b, f, :].rearrange("p (a n) -> p a n", a=2),
                                           ps[:, 2 + 2 * (f % 2):4 + 2 * (f % 2), 0:HALF],
                                           ACT.Gelu).then_inc(h_ready, 1)

            experts(0, 2)

            layer_norm(3)
            turned(3)
            for c in range(NB):
                act.wait_ge(qkv2_mm, c + 1)
                if c == 0:
                    act.wait_ge(ones_made, 1)
                copy(vaug[:, TB * c:TB * c + TB, :, 0:GR],
                     ps[:, 4 + c, :].rearrange("p (t g r) -> p t g r", t=TB, g=NG)).then_inc(v2_ready, 1)
            act.wait_ge(proj_in, 16 * 3 * GH)
            copy(flat(pstk[0:3 * GR, :, :]), flat(projf[:])).then_inc(pstk_ready, 1)
            for n in range(2):
                if n:
                    act.wait_ge(stk_in, 16 * 3 * NG)
                for c in range(NB):
                    act.wait_ge(qkv2_mm, NB * (n + 1) + c + 1)
                    copy(part_hi[:, c * BK:(c + 1) * BK], ps[:, 4 * n + c, :]).then_inc(part_ready, 1)
            for s in range(2 * NT):
                act.wait_ge(kf_mm, s + 1)
                if s >= 3:
                    act.wait_ge(kf_ready, s - 2)
                act.activation(expo[:, s % 3, :], flat(ps[:, 2 * (s % 3):2 * (s % 3) + 2, :]), ACT.Exp,
                               bias=minus_one[:]).then_inc(kf_exp, 1)
            act.wait_ge(kv_mm, 2 * NT)
            for gm in range(2):
                rows = slice(64 * gm, 64 * gm + GR + 1)
                copy(kv_sb[rows, :, :], ps[rows, 6:8, :]).then_inc(kv_copied, 1)
            act.wait_ge(kf_ready, 2 * NT)

            def query_exp(c, j):
                for gm in range(2):
                    u = c * 16 + 2 * j + gm
                    act.wait_ge(qf_mm, u + 1)
                    act.wait_ge(qf_ready, u + 1)
                    act.activation(expo[:, j % 2, gm * BK:(gm + 1) * BK], ps[:, 2 * (j % 2) + gm, :], ACT.Exp,
                                   bias=minus_one[:]).then_inc(qf_exp, 1)

            def copy_at(c):
                act.wait_ge(at_mm, c * 8 + 10)
                copy(flat(at_sb[:]), flat(ps[:, 4:6, :])).then_inc(at_ready, 1)

            def copy_attT(c):
                act.wait_ge(att_turned, c + 1)
                copy(attT[:], ps[:, 6, :]).then_inc(attT_ready, 1)

            for j in range(8):
                query_exp(0, j)
            with act.Fori(1, NB) as c:
                for j in range(8):
                    query_exp(c, j)
                    if j == 0:
                        copy_at(c - 1)
                    if j == 5:
                        copy_attT(c - 1)
            copy_at(NB - 1)
            copy_attT(NB - 1)
            experts(1, 4)

        @block.vector
        def _(dve):
            def layer_norm(n, src, dst):
                for t in range(NT):
                    if n == 0 and t % TB == 0:
                        dve.wait_ge(x_in[t // TB], 16)
                    if n == 1 and t % 2 == 0:
                        dve.wait_ge(otok_ready, t // 2 + 1)
                    dve.bn_stats(stats[:, t, :], src[:, t, :]).then_inc(ln_stat, 1)
                for t in range(NT):
                    dve.wait_ge(ln_stat, NT * n + t + 1)
                    dve.bn_aggr(mv[:, t, :], stats[:, t, :]).then_inc(ln_mv, 1)
                dve.wait_ge(ln_std, n + 1)
                dve.reciprocal(rstd[:], std[:]).then_inc(ln_rstd, 1)
                dve.wait_ge(ln_rstd, n + 1)
                for t in range(NT):
                    dve.tensor_scalar(dst[:, t, :], src[:, t, :], mv[:, t, 0:1], rstd[:, t:t + 1],
                                      ALU.subtract, ALU.mult).then_inc(ln_out, 1)

            layer_norm(0, xres, xn)
            dve.wait_ge(sel_made, 1)
            dve.tensor_copy(sel[:], sel_f[:]).then_inc(sel_made, 1)

            for c in range(NB):
                dve.wait_ge(sq_ready, c + 1)
                dve.reduce_sum(norm[:, TB * c:TB * c + TB, :],
                               squares[:, TB * c:TB * c + TB, :].rearrange("p t (g d) -> p t g d", d=HD),
                               AX_X).then_inc(sumsq, 1)
            for c in range(NB):
                tt = slice(TB * c, TB * c + TB)
                dve.wait_ge(norm_ready, c + 1)
                dve.tensor_scalar(rnorm[:, tt, :], rnorm[:, tt, :], 1e-12, None, ALU.max).then_inc(rn_clamped, 1)
                dve.wait_ge(rn_clamped, c + 1)
                dve.reciprocal(rnorm[:, tt, :], rnorm[:, tt, :]).then_inc(rn_ready, 1)
                dve.wait_ge(rn_ready, c + 1)
                qk = raw[:, tt, 0:2 * D].rearrange("p t (g d) -> p t g d", d=HD)
                dve.tensor_tensor(qk, qk, rnorm[:, tt, :].unsqueeze(3).broadcast_to((P, TB, 2 * H, HD)),
                                  ALU.mult).then_inc(unit_ready, 1)
            dve.wait_ge(beta_ready, 1)
            for c in range(NB):
                tt = slice(TB * c, TB * c + TB)
                dve.wait_ge(unit_ready, c + 1)
                dve.tensor_tensor(bk[:, tt, :].rearrange("p t (h d) -> p t h d", d=HD),
                                  raw[:, tt, D:2 * D].rearrange("p t (h d) -> p t h d", d=HD),
                                  beta[:, tt, :].unsqueeze(3).broadcast_to((P, TB, H, HD)),
                                  ALU.mult).then_inc(bk_ready, 1)
            for c in range(NB):
                cc = slice(c * BK, (c + 1) * BK)
                for n, (hi, lo) in enumerate(((khi, klo), (vhi, vlo))):
                    dve.wait_ge(hi_ready, 4 * c + n + 1)
                    dve.tensor_tensor(lo[:, cc], ps[:, 4 * (c % 2) + n, :], hi[:, cc].bitcast(F32),
                                      ALU.subtract).then_inc(lo_ready, 1)

            dve.wait_ge(qkv_turned, 4 * NB)
            dve.memset(state[:, :, CH - 1:CH], 0.0).then_inc(carry_zero, 1)
            dve.wait_ge(carry_zero, 1)

            def scan(c, i):
                dve.wait_ge(decay_ready, c * HD + i + 1)
                dve.wait_ge(update_ready, c * HD + i + 2)
                dve.wait_ge(read_ready, c * HD + i + 1)
                dve.tensor_tensor_scan(out=state[:, i, :], data0=decay[:, i % 2, :], data1=update[:, i % 2, :],
                                       initial=state[:, i, CH - 1:CH], op0=ALU.mult,
                                       op1=ALU.add).then_inc(scan_done, 1)

            with dve.Fori(0, NCH) as c:
                for i in range(HD):
                    dve.wait_ge(krep_ready, c * HD + i + 1)
                    dve.wait_ge(scan_done, c * HD + i + 1)
                    dve.tensor_tensor(decay[:, i % 2, :], flat(ps[:, 0:2, :]), bkT[:, bass.ds(c * CH, CH)],
                                      ALU.mult).then_inc(krep_used, 1)
                    dve.wait_ge(vrep_ready, c * HD + i + 1)
                    dve.tensor_tensor(update[:, i % 2, :], flat(ps[:, 2:4, :]), bkT[:, bass.ds(c * CH, CH)],
                                      ALU.mult).then_inc(update_ready, 1)
                    if i:
                        scan(c, i - 1)
                scan(c, HD - 1)

            layer_norm(1, otok, otok)
            for c in range(NB):
                cc = slice(c * BK, (c + 1) * BK)
                dve.wait_ge(nT_ready, c + 1)
                dve.wait_ge(gate_ready, c + 1)
                dve.tensor_tensor(gated[:, cc], bkT[:, cc], qT[:, cc], ALU.mult).then_inc(gated_ready, 1)
            for c in range(NB):
                dve.wait_ge(y_mm, c + 1)
                rows = flat(xres[:, TB * c:TB * c + TB, :])
                dve.tensor_tensor(rows, ps[:, 4 + c, :], rows, ALU.add).then_inc(xres_a, 1)

            def experts(k, n):
                if k == 0:
                    dve.wait_ge(xres_a, NB)
                else:
                    dve.wait_ge(xres_b, NB + 1)
                    dve.wait_ge(scattered, 16 * KT)
                layer_norm(n, xres, xn)
                def link(ins):
                    steps[0] += 1
                    ins.then_inc(route_step, 1)
                    dve.wait_ge(route_step, steps[0])

                dve.wait_ge(logit_mm, k + 1)
                dve.tensor_copy(flat(lg[:]), ps[:, 4, 0:NT * NE]).then_inc(logit_ready, 1)
                dve.wait_ge(logit_ready, k + 1)
                by_choice = lambda c: chosen[:, :, c * NT:(c + 1) * NT].rearrange("p e t -> p t e")
                wide = lambda ap: ap.unsqueeze(2).broadcast_to((P, NT, NE))
                over_e = lambda t: t[:].rearrange("p e t -> p t e")
                for c, src in enumerate((lg, lg2)):
                    link(dve.tensor_reduce(top[:, c, :], src[:], AX_X, ALU.max))
                    link(dve.tensor_tensor(ranked[:], src[:], wide(top[:, c, :]), ALU.is_equal))
                    link(dve.tensor_tensor(ranked[:], ranked[:], low_first[:], ALU.mult))
                    link(dve.tensor_reduce(best[:, c, :], ranked[:], AX_X, ALU.max))
                    link(dve.tensor_tensor(by_choice(c), ranked[:], wide(best[:, c, :]), ALU.is_equal))
                    if c == 0:
                        link(dve.scalar_tensor_tensor(out=lg2[:], in0=by_choice(0), scalar=-1e30, in1=lg[:],
                                                      op0=ALU.mult, op1=ALU.add))
                dve.tensor_copy(chosen_bf[:], flat(chosen[:])).then_inc(chosen_ready, 1)
                dve.tensor_tensor(gap[:], top[:, 0, :], top[:, 1, :], ALU.subtract).then_inc(gap_ready, 1)
                link(dve.tensor_tensor(table2[:], chosen[:], expert_base[:], ALU.mult))
                link(dve.tensor_reduce(base[:], over_e(table2), AX_X, ALU.add))
                dve.wait_ge(count_mm, k + 1)
                link(dve.tensor_tensor_scan(out=upto[:], data0=flat(first_tile[:]), data1=ps[:, 5, 0:NE * KT],
                                            initial=0.0, op0=ALU.mult, op1=ALU.add))
                link(dve.tensor_tensor(flat(table[:]), ps[:, 5, NE * KT:2 * NE * KT], upto[:], ALU.add))
                link(dve.tensor_tensor(table[:], table[:], chosen[:], ALU.mult))
                link(dve.tensor_reduce(rank[:], over_e(table), AX_X, ALU.add))
                link(dve.tensor_single_scalar(kept[:], rank[:], float(CAP), ALU.is_lt))
                link(dve.tensor_tensor(slot[:], rank[:], base[:], ALU.add))
                link(dve.scalar_tensor_tensor(out=slot2[:], in0=kept[:], scalar=-FAR, in1=slot[:],
                                              op0=ALU.mult, op1=ALU.add))
                dve.tensor_scalar(put_at[:], slot2[:], FAR, None, ALU.add).then_inc(index_ready, 1)
                dve.wait_ge(prob_ready, 2 * k + 2)
                dve.tensor_tensor(weight[:], prob[:], kept[:], ALU.mult).then_inc(weight_ready, 1)

                def outputs(e, b, used):
                    s = k * NE + e + b
                    dve.wait_ge(ye_mm, s + 3)
                    if used:
                        dve.wait_ge(ye_out[b], 16 * NS * (NE // 2) * k + e * (8 * NS))
                    dve.wait_ge(xe_in[b], 16 * (NE // 2) * k + e * 8 + 16)
                    dve.tensor_copy(y_to[:, b, :], xe[:, b, :, D].bitcast(I32)).then_inc(y_to_ready, 1)
                    dve.wait_ge(y_to_ready, s + 1)
                    dve.tensor_copy(ye[:, b, :], flat(ps[:, 6:8, :])[:, 0:NS * D]).then_inc(ye_ready, 1)

                for b in range(2):
                    outputs(0, b, k > 0)
                with dve.Fori(1, NE // 2) as pair:
                    for b in range(2):
                        outputs(pair * 2, b, True)

                dve.wait_ge(weight_ready, k + 1)

                def second(t):
                    dve.wait_ge(mix_first, k * NT + t + 1)
                    dve.scalar_tensor_tensor(out=xres[:, t, :], in0=got[:, NT + t, :],
                                             scalar=weight[:, NT + t:NT + t + 1], in1=xres[:, t, :],
                                             op0=ALU.mult, op1=ALU.add).then_inc(mixed, 1)

                for t in range(NT):
                    if t % TB == 0:
                        dve.wait_ge(got_in[t // TB], 32 * (k + 1))
                    dve.scalar_tensor_tensor(out=xres[:, t, :], in0=got[:, t, :], scalar=weight[:, t:t + 1],
                                             in1=xres[:, t, :], op0=ALU.mult, op1=ALU.add).then_inc(mix_first, 1)
                    if t:
                        second(t - 1)
                second(NT - 1)

            steps = [0]
            experts(0, 2)

            dve.wait_ge(mixed, NT)
            dve.wait_ge(scattered, 16 * KT)
            layer_norm(3, xres, xn)
            dve.wait_ge(pstk_ready, 1)
            lo = slice(2 * GR, 3 * GR)
            dve.tensor_tensor(flat(pstk[lo, :, :]), flat(projf[lo, :, :]), flat(pstk[lo, :, :]).bitcast(F32),
                              ALU.subtract).then_inc(pstklo_ready, 1)
            for n in range(2):
                if n:
                    dve.wait_ge(stk_in, 16 * 3 * NG)
                for c in range(NB):
                    cc = slice(c * BK, (c + 1) * BK)
                    dve.wait_ge(part_ready, NB * n + c + 1)
                    dve.tensor_tensor(part_lo[:, cc], ps[:, 4 * n + c, :], part_hi[:, cc].bitcast(F32),
                                      ALU.subtract).then_inc(partlo_ready, 1)
            for s in range(2 * NT):
                dve.wait_ge(kf_exp, s + 1)
                if s >= 3:
                    dve.wait_ge(kv_mm, s - 2)
                dve.scalar_tensor_tensor(out=feat[:, s % 3, :], in0=expo[:, s % 3, :], scalar=1.0,
                                         in1=flat(ps[:, 2 * (s % 3):2 * (s % 3) + 2, :]), op0=ALU.min,
                                         op1=ALU.max).then_inc(kf_ready, 1)
            dve.wait_ge(kv_turned, 1)
            dve.wait_ge(ones_made, 1)
            heads = ps[:, 4:6, :].rearrange("p m (q a c) -> p q m a c", q=2, a=GH)
            kvl_v = kvl[:].rearrange("p (q m a) c -> p q m a c", q=2, m=2)
            for a_ in range(GH):
                cols = slice(HD * a_, HD * (a_ + 1))
                dve.tensor_copy(kvl_v[:, :, :, a_, cols], heads[:, :, :, a_, cols]).then_inc(kvl_ready, 1)
                dve.tensor_copy(kvl_v[:, :, :, a_, GR + a_:GR + a_ + 1],
                                heads[:, :, :, a_, GR:GR + 1]).then_inc(kvl_ready, 1)
            dve.wait_ge(kv_mm, 2 * NT)

            def query_feat(c, j):
                dve.wait_ge(at_mm, c * 8 + j + 1)
                for gm in range(2):
                    cc = slice(gm * BK, (gm + 1) * BK)
                    dve.wait_ge(qf_exp, c * 16 + 2 * j + gm + 1)
                    dve.scalar_tensor_tensor(out=feat[:, j % 2, cc], in0=expo[:, j % 2, cc], scalar=1.0,
                                             in1=ps[:, 2 * (j % 2) + gm, :], op0=ALU.min,
                                             op1=ALU.max).then_inc(qf_ready, 1)

            def divide(c):
                dve.wait_ge(at_turned, c + 1)
                by_tok = flat(ps[:, 6:8, :]).rearrange("p (t g r) -> p t g r", t=TB, g=NG)
                dve.tensor_scalar(den[:].rearrange("p t (g a) -> p t g a", g=NG),
                                  by_tok[:, :, :, GR:GR + GH], 1e-8, None, ALU.add).then_inc(den_ready, 1)
                dve.wait_ge(den_ready, c + 1)
                dve.reciprocal(rden[:], den[:]).then_inc(rden_ready, 1)
                dve.wait_ge(rden_ready, c + 1)
                for t in range(TB):
                    dve.tensor_tensor(
                        att[:, t, :].rearrange("p (g a d) -> p g a d", g=NG, a=GH),
                        by_tok[:, t, :, 0:GR].rearrange("p g (a d) -> p g a d", a=GH),
                        rden[:, t, :].rearrange("p (g a) -> p g a", g=NG).unsqueeze(3).broadcast_to(
                            (P, NG, GH, HD)), ALU.mult).then_inc(att_ready, 1)

            def add_b(c):
                dve.wait_ge(o2_mm, c + 1)
                rows = flat(xres[:, bass.ds(c * TB, TB), :])
                dve.tensor_tensor(rows, ps[:, 7, :], rows, ALU.add).then_inc(xres_b, 1)

            for j in range(8):
                query_feat(0, j)
            with dve.Fori(1, NB) as c:
                for j in range(8):
                    query_feat(c, j)
                    if j == 2:
                        divide(c - 1)
                    if j == 7:
                        add_b(c - 1)
            divide(NB - 1)
            add_b(NB - 1)

            experts(1, 4)

        @block.tensor
        def _(pe):
            def mm(o, lhsT, rhs, start=True, stop=True, **kw):
                return pe.matmul(o, lhsT, rhs, start=start, stop=stop, **kw)

            def turn(n, base):
                src = otok if n == 1 else xn
                for t in range(NT):
                    pe.wait_ge(ln_out, NT * base + t + 1)
                    ins = pe.transpose(ps[:, t // TB, (t % TB) * P:(t % TB + 1) * P], src[:, t, :], ident[:])
                    if t % TB == TB - 1:
                        ins.then_inc(xn_turned, 1)

            pe.wait_ge(const_made, N_CONST)
            pe.wait_ge(wnat_in, 32)
            for n in range(4):
                ins = pe.transpose(ps[:, 4, n * D:(n + 1) * D], wnat[:, n, :], ident[:])
            ins.then_inc(wT_mm, 1)
            turn(0, 0)
            pe.wait_ge(w_in, 16 * 10)
            pe.wait_ge(wT_ready, 4)
            for t in range(NT):
                pe.wait_ge(xnT_ready, t // TB + 1)
                if t >= 4:
                    pe.wait_ge(raw_ready, t - 3)
                mm(ps[:, 4 + t % 4, 0:QKVB], xnT[:, t * P:(t + 1) * P], wall[:]).then_inc(qkv_mm, 1)
            pe.wait_ge(raw_ready, NT)
            for c in range(NB):
                pe.wait_ge(bk_ready, c + 1)
                if c >= 2:
                    pe.wait_ge(hi_ready, 4 * (c - 1))
                    pe.wait_ge(lo_ready, 2 * (c - 1))
                for n in range(4):
                    for t in range(TB):
                        tile = TB * c + t
                        src = (raw[:, tile, D:2 * D], raw[:, tile, 2 * D:3 * D], raw[:, tile, 0:D], bk[:, tile, :])[n]
                        ins = pe.transpose(ps[:, 4 * (c % 2) + n, t * P:(t + 1) * P], src, ident[:])
                    ins.then_inc(qkv_turned, 1)

            pe.wait_ge(hi_ready, 4 * NB)
            pe.wait_ge(lo_ready, 2 * NB)
            pe.wait_ge(sel_made, 2)

            def repeat(c, i, bank, hi, lo, done):
                for h in range(2):
                    cols = bass.ds(c * CH + h * BK, BK)
                    mm(ps[:, bank + h, :], sel[:, i, :], hi[:, cols], stop=False)
                    ins = mm(ps[:, bank + h, :], sel[:, i, :], lo[:, cols], start=False)
                ins.then_inc(done, 1)

            def sum_rows(c, ib):
                pe.wait_ge(read_ready, c * HD + HD + 4 * ib + 4)
                pe.wait_ge(oT_ready, c * 2 + ib + 1)
                for h in range(2):
                    for im in range(4):
                        ins = mm(ps[32 * im:32 * im + 32, 4 + 2 * ib + h, :], headsum[:],
                                 read[:, 4 * ib + im, h * BK:(h + 1) * BK], tile_position=(0, 32 * im))
                ins.then_inc(out_ready, 1)

            with pe.Fori(0, NCH) as c:
                for i in range(HD):
                    pe.wait_ge(krep_used, c * HD + i + 1)
                    repeat(c, i, 0, khi, klo, krep_ready)
                    pe.wait_ge(update_ready, c * HD + i + 1)
                    repeat(c, i, 2, vhi, vlo, vrep_ready)
                    if i == 6:
                        sum_rows(c, 0)
                sum_rows(c, 1)

            pe.wait_ge(oT_ready, 2 + 2 * NCH)
            for c in range(NB):
                mm(ps[:, 4 + c, :], wgate[:], xnT[:, c * BK:(c + 1) * BK]).then_inc(gate_mm, 1)
            pe.wait_ge(krep_used, HD * NCH + 1)
            pe.wait_ge(update_ready, HD * NCH + 1)
            for c in range(2 * NB):
                if c >= 4:
                    pe.wait_ge(otok_ready, c - 3)
                for t in range(2):
                    for ib in range(2):
                        col = (2 * t + ib) * P
                        ins = pe.transpose(ps[:, c % 4, col:col + P],
                                           oT[:, ib, (2 * c + t) * P:(2 * c + t + 1) * P], ident[:])
                ins.then_inc(o_turned, 1)
            pe.wait_ge(otok_ready, 2 * NB)
            turn(1, 1)
            pe.wait_ge(gate_ready, NB)
            for c in range(NB):
                pe.wait_ge(gated_ready, c + 1)
                for t in range(TB):
                    ins = mm(ps[:, 4 + c, t * P:(t + 1) * P], gated[:, (TB * c + t) * P:(TB * c + t + 1) * P], wout[:])
                ins.then_inc(y_mm, 1)

            def experts(k, n):
                turn(n, n)
                pe.wait_ge(ye_ready, k * NE + 1)
                for t in range(NT):
                    pe.wait_ge(xnT_ready, (n - 1 if n < 2 else n - 1) * NB + t // TB + 1)
                    ins = mm(ps[:, 4, t * NE:(t + 1) * NE], xnT[:, t * P:(t + 1) * P], wg_sb[:])
                ins.then_inc(logit_mm, 1)
                pe.wait_ge(chosen_ready, k + 1)
                mm(ps[:, 5, 0:NE * KT], ones_bf[:], chosen_bf[:])
                mm(ps[:, 5, NE * KT:2 * NE * KT], before_bf[:], chosen_bf[:]).then_inc(count_mm, 1)
                pe.wait_ge(cproj_in, 16)
                with pe.Fori(0, NE // 2) as pair:
                    for b in range(2):
                        e = pair * 2
                        s = k * NE + e + b
                        pe.wait_ge(xe_in[b], 16 * (NE // 2) * k + e * 8 + 16)
                        pe.wait_ge(xeT_ready, s + 1)
                        for i in range(NS):
                            ins = pe.transpose(ps[:, i // TB, (i % TB) * P:(i % TB + 1) * P], xe[:, b, i, 0:D],
                                               ident[:])
                        ins.then_inc(xe_turned, 1)
                        pe.wait_ge(wfc_ready, s + 1)
                        pe.wait_ge(xeT_ready, s + 2)
                        for f in range(NF):
                            pe.wait_ge(h_ready, s * NF + f + 1)
                            for a_ in range(2):
                                ins = mm(ps[:, 2 + 2 * (f % 2) + a_, 0:HALF], wfc[:, b, f * P:(f + 1) * P],
                                         xeT[:, b, a_ * HALF:(a_ + 1) * HALF])
                            ins.then_inc(h_mm, 1)
                        pe.wait_ge(h_ready, s * NF + NF + 2)
                        pe.wait_ge(ye_ready, s + 1)
                        for i in range(NS):
                            for f in range(NF):
                                ins = mm(ps[:, 6 + i // TB, (i % TB) * P:(i % TB + 1) * P],
                                         hT[:, b, f, i * P:(i + 1) * P], cproj_sb[:, bass.ds(e + b, 1), f, :],
                                         start=f == 0, stop=f == NF - 1)
                        ins.then_inc(ye_mm, 1)

            experts(0, 2)

            turn(3, 3)
            for t in range(NT):
                pe.wait_ge(xnT_ready, 2 * NB + t // TB + 1)
                ins = mm(ps[:, 4 + t // TB, (t % TB) * P:(t % TB + 1) * P], xnT[:, t * P:(t + 1) * P], wvT[:])
                if t % TB == TB - 1:
                    ins.then_inc(qkv2_mm, 1)
            for c in range(NB):
                mm(ps[:, c, :], wkT[:], xnT[:, c * BK:(c + 1) * BK]).then_inc(qkv2_mm, 1)
            for c in range(NB):
                pe.wait_ge(v2_ready, c + 1)
                mm(ps[:, 4 + c, :], wqT[:], xnT[:, c * BK:(c + 1) * BK]).then_inc(qkv2_mm, 1)

            def key_features(s):
                t, gp = divmod(s, 2)
                if s >= 3:
                    pe.wait_ge(kf_ready, s - 2)
                for gm in range(2):
                    g = 2 * gp + gm
                    ins = mm(ps[:, 2 * (s % 3) + gm, :], kstk[:, g, t * P:(t + 1) * P], pstk[:, g, :])
                ins.then_inc(kf_mm, 1)

            pe.wait_ge(stk_in, 16 * 3 * NG)
            pe.wait_ge(ones_made, 4)
            pe.wait_ge(pstklo_ready, 1)
            pe.wait_ge(partlo_ready, 2 * NB)
            for s in range(3):
                key_features(s)
            for s in range(2 * NT):
                t, gp = divmod(s, 2)
                pe.wait_ge(kf_ready, s + 1)
                for gm in range(2):
                    ins = mm(ps[64 * gm:64 * gm + GR + 1, 6 + gp, :], vaug[:, t, 2 * gp + gm, :],
                             feat[:, s % 3, gm * BK:(gm + 1) * BK], start=t == 0, stop=t == NT - 1,
                             tile_position=(0, 64 * gm))
                ins.then_inc(kv_mm, 1)
                if s + 3 < 2 * NT:
                    key_features(s + 3)
            for gm in range(2):
                rows = slice(64 * gm, 64 * gm + GR + 1)
                pe.wait_ge(kv_copied, gm + 1)
                for n in range(2 * GH):
                    gp, a_ = divmod(n, GH)
                    ins = pe.transpose(ps[:, 4 + gm, n * 64:n * 64 + GR + 1],
                                       kv_sb[rows, gp, a_ * F:(a_ + 1) * F], ident[rows, rows])
            ins.then_inc(kv_turned, 1)

            def query_features(c, j):
                gp, a_ = divmod(j, GH)
                for gm in range(2):
                    g = 2 * gp + gm
                    pe.wait_ge(qf_ready, c * 16 + 2 * j + gm + 1)
                    mm(ps[:, 2 * (j % 2) + gm, :], pstk[:, g, a_ * F:(a_ + 1) * F],
                       qstk[:, g, bass.ds(c * BK, BK)]).then_inc(qf_mm, 1)

            pe.wait_ge(stk_in, 2 * 16 * 3 * NG)
            pe.wait_ge(kvl_ready, 2 * GH)
            def attend(c, j):
                gp, a_ = divmod(j, GH)
                for gm in range(2):
                    h = (2 * gp + gm) * GH + a_
                    ins = mm(ps[64 * gm:64 * gm + 64, 4 + gp, :], kvl[:, h, :],
                             feat[:, j % 2, gm * BK:(gm + 1) * BK], start=a_ == 0, stop=a_ == GH - 1,
                             tile_position=(0, 64 * gm))
                ins.then_inc(at_mm, 1)

            def turn_at(c):
                pe.wait_ge(at_ready, c + 2)
                pe.wait_ge(xres_b, c + 1)
                for t in range(TB):
                    for gp in range(2):
                        col = (2 * (t % 2) + gp) * P
                        ins = pe.transpose(ps[:, 6 + t // 2, col:col + P], at_sb[:, gp, t * P:(t + 1) * P],
                                           ident[:])
                ins.then_inc(at_turned, 1)

            def turn_att(c):
                pe.wait_ge(att_ready, c * TB + TB)
                for t in range(TB):
                    ins = pe.transpose(ps[:, 6, t * P:(t + 1) * P], att[:, t, :], ident[:])
                ins.then_inc(att_turned, 1)

            def out_b(c):
                pe.wait_ge(attT_ready, c + 1)
                for t in range(TB):
                    mm(ps[:, 7, t * P:(t + 1) * P], attT[:, t * P:(t + 1) * P], woT[:], stop=False)
                    ins = mm(ps[:, 7, t * P:(t + 1) * P], ones_row[:], bout_row[:], start=False)
                ins.then_inc(o2_mm, 1)

            def chunk(c, first=False, final=False):
                for j in range(8):
                    if j < 6:
                        query_features(c, j + 2)
                    elif not final:
                        query_features(c + 1, j - 6)
                    if j == 0:
                        pe.wait_ge(at_ready, c + 1)
                    pe.wait_ge(qf_ready, c * 16 + 2 * j + 6)
                    attend(c, j)
                    if not first:
                        if j == 0:
                            turn_at(c - 1)
                        if j == 4:
                            turn_att(c - 1)
                        if j == 6:
                            out_b(c - 1)

            query_features(0, 0)
            query_features(0, 1)
            chunk(0, first=True)
            with pe.Fori(1, NB - 1) as c:
                chunk(c)
            chunk(NB - 1, final=True)
            turn_at(NB - 1)
            turn_att(NB - 1)
            out_b(NB - 1)

            experts(1, 4)


_INS = ["L0_attn_a_x", "L0_attn_a_Wq", "L0_attn_a_Wk", "L0_attn_a_Wv", "L0_attn_a_Wbeta", "L0_attn_a_Wg",
        "L0_attn_a_Wout", "L0_attn_a_ln_g", "L0_attn_a_ln_b", "L0_attn_b_W_qkv", "L0_attn_b_proj",
        "L0_attn_b_W_out", "L0_attn_b_b_out", "L0_ffn_w_g", "L0_ffn_c_fc", "L0_ffn_c_proj"]


def kernel(**inputs):
    import numpy as np
    import concourse.bacc as bacc
    from concourse.bass_utils import run_bass_kernel_spmd

    nc = bacc.Bacc("TRN2", target_bir_lowering=False, num_devices=1)
    arrays, args = {}, []
    for name in _INS:
        a = np.ascontiguousarray(inputs[name])
        arrays["in_" + name] = a
        args.append(nc.dram_tensor("in_" + name, a.shape, mybir.dt.from_np(a.dtype), kind="ExternalInput").ap())
    out = nc.dram_tensor("out_0", (1, TOK, D), F32, kind="ExternalOutput").ap()
    program(nc, *args, out)
    r = run_bass_kernel_spmd(nc, [arrays], core_ids=[0])
    return r.results[0]["out_0"]
```
